# Optimizing a Trainium2 kernel written in Bass

```python
import numpy as np
import jax
import jax.numpy as jnp

def _softmax(x, axis=-1):
    return jax.nn.softmax(x, axis=axis)

def _gelu(x):
    return jax.nn.gelu(x, approximate=True)

def _silu(x):
    return jax.nn.silu(x)

def _sigmoid(x):
    return jax.nn.sigmoid(x)

def _layernorm(x, axis=-1, eps=1e-05):
    m = jnp.mean(x, axis=axis, keepdims=True)
    v = jnp.var(x, axis=axis, keepdims=True)
    return (x - m) / jnp.sqrt(v + eps)

def _scatter_add(tgt, idx, src, axis=0):
    return tgt.at[idx].add(src)

def _segment_sum(src, seg, n):
    return jax.ops.segment_sum(src, seg, n)
kernel_name = 'mk_seq_preln_d1_jaxref_r4_bbb792'

def setup_inputs(seed: int=0):
    np.random.seed(seed)
    _w = jnp.asarray

    def _L0_attn_setup():
        import jax, jax.numpy as jnp
        import numpy as np
        import math
        H = 512
        B = 4
        T = 512
        LAYERS = 24
        INDEX = 3
        EPS = 1e-05

        def _layer_norm(x, g, b):
            m = jnp.mean(x, axis=-1, keepdims=True)
            v = jnp.mean((x - m) ** 2, axis=-1, keepdims=True)
            return (x - m) * jax.lax.rsqrt(v + EPS) * g + b

        def _time_shift(x):
            return jnp.pad(x, ((0, 0), (1, 0), (0, 0)))[:, :-1, :]

        def _wkv_run(k, v, tm_first, tm_decay):
            C = k.shape[-1]
            aa = jnp.zeros((C,), k.dtype)
            bb = jnp.zeros((C,), k.dtype)
            pp = jnp.full((C,), -1e+38, k.dtype)
            ww = tm_first + k
            p = jnp.maximum(pp, ww)
            e1 = jnp.exp(pp - p)
            e2 = jnp.exp(ww - p)
            a = e1 * aa + e2 * v
            b = e1 * bb + e2
            return a / b
        key = jax.random.key(seed)
        ks = jax.random.split(key, 9)
        i = jnp.arange(H, dtype=jnp.float32)
        r01 = INDEX / (LAYERS - 1)
        r1pz = 1.0 - INDEX / LAYERS
        tm_decay = -5.0 + 8.0 * (i / (H - 1)) ** (0.7 + 1.3 * r01)
        zigzag = ((jnp.arange(H) + 1) % 3 - 1).astype(jnp.float32) * 0.5
        tm_first = jnp.float32(math.log(0.3)) + zigzag
        xr = i / H
        tm_mk = (xr ** r1pz)[None, None, :]
        tm_mv = tm_mk + 0.3 * r01
        tm_mr = (xr ** (0.5 * r1pz))[None, None, :]
        cm_mk = (xr ** r1pz)[None, None, :]
        cm_mr = (xr ** r1pz)[None, None, :]
        s = 1.0 / math.sqrt(H)
        s4 = 1.0 / math.sqrt(4 * H)
        Wk = jax.random.normal(ks[0], (H, H), jnp.float32) * s
        Wv = jax.random.normal(ks[1], (H, H), jnp.float32) * s
        Wr = jax.random.normal(ks[2], (H, H), jnp.float32) * s
        Wo = jax.random.normal(ks[3], (H, H), jnp.float32) * s
        Wkey = jax.random.normal(ks[4], (4 * H, H), jnp.float32) * s
        Wval = jax.random.normal(ks[5], (H, 4 * H), jnp.float32) * s4
        Wcr = jax.random.normal(ks[6], (H, H), jnp.float32) * s
        x = jax.random.normal(ks[7], (B, T, H), jnp.float32)
        return {'x': x, 'ln1_g': jnp.ones((H,), jnp.float32), 'ln1_b': jnp.zeros((H,), jnp.float32), 'ln2_g': jnp.ones((H,), jnp.float32), 'ln2_b': jnp.zeros((H,), jnp.float32), 'tm_decay': tm_decay, 'tm_first': tm_first, 'tm_mk': tm_mk, 'tm_mv': tm_mv, 'tm_mr': tm_mr, 'Wk': Wk, 'Wv': Wv, 'Wr': Wr, 'Wo': Wo, 'cm_mk': cm_mk, 'cm_mr': cm_mr, 'Wkey': Wkey, 'Wval': Wval, 'Wcr': Wcr}
    _L0_attn_in = _L0_attn_setup()

    def _L0_ffn_setup():
        import jax, jax.numpy as jnp
        import numpy as np
        HIDDEN = 512
        INTER = 2048
        BATCH, LOCAL_SEQ = (2, 1024)
        key = jax.random.key(seed)
        k1, k2, k3 = jax.random.split(key, 3)
        h_shard = jax.random.normal(k1, (BATCH, LOCAL_SEQ, HIDDEN), dtype=jnp.float32)
        w_gate_up = jax.random.normal(k2, (2 * INTER, HIDDEN), dtype=jnp.float32) * 0.02
        w_down = jax.random.normal(k3, (HIDDEN, INTER), dtype=jnp.float32) * 0.02
        return {'h_shard': h_shard, 'w_gate_up': w_gate_up, 'w_down': w_down}
    _L0_ffn_in = _L0_ffn_setup()
    _d = {'L0_attn_x': _L0_attn_in['x'], 'L0_attn_ln1_g': _L0_attn_in['ln1_g'], 'L0_attn_ln1_b': _L0_attn_in['ln1_b'], 'L0_attn_ln2_g': _L0_attn_in['ln2_g'], 'L0_attn_ln2_b': _L0_attn_in['ln2_b'], 'L0_attn_tm_decay': _L0_attn_in['tm_decay'], 'L0_attn_tm_first': _L0_attn_in['tm_first'], 'L0_attn_tm_mk': _L0_attn_in['tm_mk'], 'L0_attn_tm_mv': _L0_attn_in['tm_mv'], 'L0_attn_tm_mr': _L0_attn_in['tm_mr'], 'L0_attn_Wk': _L0_attn_in['Wk'], 'L0_attn_Wv': _L0_attn_in['Wv'], 'L0_attn_Wr': _L0_attn_in['Wr'], 'L0_attn_Wo': _L0_attn_in['Wo'], 'L0_attn_cm_mk': _L0_attn_in['cm_mk'], 'L0_attn_cm_mr': _L0_attn_in['cm_mr'], 'L0_attn_Wkey': _L0_attn_in['Wkey'], 'L0_attn_Wval': _L0_attn_in['Wval'], 'L0_attn_Wcr': _L0_attn_in['Wcr'], 'L0_ffn_w_gate_up': _L0_ffn_in['w_gate_up'], 'L0_ffn_w_down': _L0_ffn_in['w_down']}
    _x0 = _d['L0_attn_x']
    _d['L0_attn_x'] = jax.random.normal(jax.random.fold_in(jax.random.key(seed), 1), (1, 2048, 512), dtype=_x0.dtype)
    del _x0
    return _d

def reference(L0_attn_x, L0_attn_ln1_g, L0_attn_ln1_b, L0_attn_ln2_g, L0_attn_ln2_b, L0_attn_tm_decay, L0_attn_tm_first, L0_attn_tm_mk, L0_attn_tm_mv, L0_attn_tm_mr, L0_attn_Wk, L0_attn_Wv, L0_attn_Wr, L0_attn_Wo, L0_attn_cm_mk, L0_attn_cm_mr, L0_attn_Wkey, L0_attn_Wval, L0_attn_Wcr, L0_ffn_w_gate_up, L0_ffn_w_down):

    def _L0_attn_ref(x, ln1_g, ln1_b, ln2_g, ln2_b, tm_decay, tm_first, tm_mk, tm_mv, tm_mr, Wk, Wv, Wr, Wo, cm_mk, cm_mr, Wkey, Wval, Wcr):
        import jax, jax.numpy as jnp
        import numpy as np
        import math
        H = 512
        B = 4
        T = 512
        LAYERS = 24
        INDEX = 3
        EPS = 1e-05

        def _layer_norm(x, g, b):
            m = jnp.mean(x, axis=-1, keepdims=True)
            v = jnp.mean((x - m) ** 2, axis=-1, keepdims=True)
            return (x - m) * jax.lax.rsqrt(v + EPS) * g + b

        def _time_shift(x):
            return jnp.pad(x, ((0, 0), (1, 0), (0, 0)))[:, :-1, :]

        def _wkv_run(k, v, tm_first, tm_decay):
            C = k.shape[-1]
            aa = jnp.zeros((C,), k.dtype)
            bb = jnp.zeros((C,), k.dtype)
            pp = jnp.full((C,), -1e+38, k.dtype)
            ww = tm_first + k
            p = jnp.maximum(pp, ww)
            e1 = jnp.exp(pp - p)
            e2 = jnp.exp(ww - p)
            a = e1 * aa + e2 * v
            b = e1 * bb + e2
            return a / b
        h = _layer_norm(x, ln1_g, ln1_b)
        hh = _time_shift(h)
        k = (h * tm_mk + hh * (1 - tm_mk)) @ Wk.T
        v = (h * tm_mv + hh * (1 - tm_mv)) @ Wv.T
        r = (h * tm_mr + hh * (1 - tm_mr)) @ Wr.T
        wkv = _wkv_run(k, v, tm_first, tm_decay)
        x = x + jax.nn.sigmoid(r) * wkv @ Wo.T
        h = _layer_norm(x, ln2_g, ln2_b)
        hh = _time_shift(h)
        kk = (h * cm_mk + hh * (1 - cm_mk)) @ Wkey.T
        kv = jax.nn.silu(kk) @ Wval.T
        sr = jax.nn.sigmoid((h * cm_mr + hh * (1 - cm_mr)) @ Wcr.T)
        x = x + sr * kv
        return x

    def _L0_ffn_ref(h_shard, w_gate_up, w_down):
        import jax, jax.numpy as jnp
        import numpy as np
        HIDDEN = 512
        INTER = 2048
        BATCH, LOCAL_SEQ = (2, 1024)
        batch, local_seq, hidden = h_shard.shape
        gate_up = jnp.einsum('bsh,oh->bso', h_shard, w_gate_up)
        gate, up = jnp.split(gate_up, 2, axis=-1)
        h = jax.nn.silu(gate) * up
        out = jnp.einsum('bsi,hi->bsh', h, w_down)
        return out
    x = L0_attn_x
    x = x + _L0_attn_ref(_layernorm(x, axis=-1), L0_attn_ln1_g, L0_attn_ln1_b, L0_attn_ln2_g, L0_attn_ln2_b, L0_attn_tm_decay, L0_attn_tm_first, L0_attn_tm_mk, L0_attn_tm_mv, L0_attn_tm_mr, L0_attn_Wk, L0_attn_Wv, L0_attn_Wr, L0_attn_Wo, L0_attn_cm_mk, L0_attn_cm_mr, L0_attn_Wkey, L0_attn_Wval, L0_attn_Wcr)
    x = x + _L0_ffn_ref(_layernorm(x, axis=-1), L0_ffn_w_gate_up, L0_ffn_w_down)
    return x

_drawn_inputs = setup_inputs


def setup_inputs(seed=0):
    import zlib

    import numpy as np

    out = dict(_drawn_inputs(seed))
    spreads = {'L0_attn_ln1_g': (1.0, 0.2),
     'L0_attn_ln1_b': (0.0, 0.316),
     'L0_attn_ln2_g': (1.0, 0.6),
     'L0_attn_ln2_b': (0.0, 0.495)}
    factors = {}
    for name, (base, spread) in spreads.items():
        noise = np.random.default_rng([zlib.crc32(name.encode()), seed]).standard_normal(out[name].shape)
        drawn = base * np.exp(spread * noise) if base else spread * noise
        out[name] = jnp.asarray(drawn.astype(out[name].dtype))
    for name, factor in factors.items():
        out[name] = (out[name] * factor).astype(out[name].dtype)
    return out
```

```python
from contextlib import ExitStack

import concourse.bass as bass
from concourse import mybir

ALU = mybir.AluOpType
ACT = mybir.ActivationFunctionType
F32 = mybir.dt.float32
F32R = mybir.dt.float32r

P = 128
H = 512
INNER = 2048
TOKENS = 2048
KT = H // P
BT = 512
BLOCKS = TOKENS // BT
SUBS = BT // P
EPS = 1e-5
NO_STATE = 1e38

GROUP = 2
GROUPS = INNER // (GROUP * P)
UNITS = GROUPS * BLOCKS
PAIR = 2 * BLOCKS
TURNS = GROUPS // 2 - 1

MATRIX = KT
CM_PIECES = 2 * GROUP
FFN_PIECES = 3 * GROUP
ITEM_R, ITEM_K, ITEM_V, ITEM_O, ITEM_CR = (n * MATRIX for n in range(5))
ITEM_X = 5 * MATRIX
ITEM_CM = ITEM_X + BLOCKS * SUBS
ITEM_FFN = ITEM_CM + GROUPS * CM_PIECES
ITEMS = ITEM_FFN + GROUPS * FFN_PIECES
STAGES = 2


def piece(item):
    return item if item < ITEM_X else item - BLOCKS * SUBS


ROW_R, ROW_K, ROW_V, ROW_O, ROW_CR = 0, 4, 8, 12, 0
ROW_ACT = 12


def row_cm(group):
    return 4 + CM_PIECES * (group % 2)


def row_ffn(group):
    return FFN_PIECES * (group % 2)


ORDER = ([(m, b) for b in range(BLOCKS) for m in ("r", "k")] + [("v", b) for b in range(BLOCKS)]
         + [("y", b) for b in range(BLOCKS)]
         + [("cr", 0), ("cr", 1), ("cr", 2), ("ck", 0), ("cr", 3), ("ck", 1), ("ck", 2), ("ck", 3)])
OPERANDS = KT * len(ORDER)
RING = 4


def operand_at(kind, b):
    return KT * ORDER.index((kind, b))


def slot_of(kind, b):
    return {"r": 2 * b, "k": 2 * b + 1}.get(kind, b) % BLOCKS


VECTORS = ["ln1_g", "ln1_b", "ln2_g", "ln2_b", "tm_first", "tm_mr", "tm_mk", "tm_mv", "cm_mr", "cm_mk"]
MIXES = {"r": 0, "k": 1, "v": 2, "cr": 3, "ck": 4}


def build(nc, x, wts, vectors, identity, out):
    x_blocks = x.rearrange("o (b s p) h -> (o b) p s h", p=P, s=SUBS)
    out_blocks = out.rearrange("o (b s p) h -> (o b) p s h", p=P, s=SUBS)

    with ExitStack() as ctx:
        def sb(name, shape, dt=F32):
            return ctx.enter_context(nc.sbuf_tensor(name, shape, dt))

        def sem(name):
            return ctx.enter_context(nc.semaphore(name))

        operand = sb("operand", [P, BLOCKS, KT, 2, BT], F32R)
        weights = sb("weights", [P, 16, 2, 512], F32R)
        feat = sb("feat", [P, KT, BLOCKS, 1 + BT])
        resid = sb("resid", [P, BLOCKS, SUBS, H])
        made = sb("made", [P, RING, BT])
        e2 = sb("e2", [P, BT])
        staging = sb("staging", [P, STAGES, 512])
        ident = sb("ident", [P, P])
        vec = sb("vec", [P, len(VECTORS), KT])
        rest = sb("rest", [P, len(MIXES), KT])
        bonus = sb("bonus", [P, KT])
        moments = sb("moments", [P, SUBS, 6])
        stats1 = sb("stats1", [P, BLOCKS, SUBS, 2])
        stats2 = sb("stats2", [P, SUBS, 2])
        var_eps = sb("var_eps", [P, SUBS])
        rstd = sb("rstd", [P, BLOCKS, SUBS])
        rstd_both = sb("rstd_both", [P, SUBS])
        rstd2 = sb("rstd2", [P, SUBS])
        scratch = sb("scratch", [P, 4, SUBS])
        minus_half = sb("minus_half", [P, SUBS])
        eps = sb("eps", [P, SUBS])

        bank = [ctx.enter_context(nc.psum_tensor(f"bank{i}", [P, 512], F32)) for i in range(8)]
        A, B = bank[:4], bank[4:]

        def token_tile(b, s):
            return feat[:, s, b, 1:1 + BT]

        def inner(u, i, part):
            return weights[:, ROW_ACT + GROUP * (u % 2) + i, part, :]

        vec_loaded, ident_loaded = sem("vec_loaded"), sem("ident_loaded")
        x_loaded = [sem(f"x_loaded{b}") for b in range(BLOCKS)]
        x_again = [sem(f"x_again{b}") for b in range(BLOCKS)]
        staged = [sem(f"staged{n}") for n in range(STAGES)]
        w_hi = sem("w_hi")
        item_done = sem("item_done")
        const_done = sem("const_done")
        pool_const = sem("pool_const")
        ln_moments, ln_stats, ln_var = sem("ln_moments"), sem("ln_stats"), sem("ln_var")
        ln_rstd, ln_step = sem("ln_rstd"), sem("ln_step")
        z1_ready, t1_psum, h1_ready = sem("z1_ready"), sem("t1_psum"), sem("h1_ready")
        edge_ready = sem("edge_ready")
        rest_part = sem("rest_part")
        op_made, op_hi, op_lo = sem("op_made"), sem("op_hi"), sem("op_lo")
        r_psum, k_psum, v_psum = sem("r_psum"), sem("k_psum"), sem("v_psum")
        r_gate, k_low, e2_ready, e2_inv = sem("r_gate"), sem("k_low"), sem("e2_ready"), sem("e2_inv")
        g_e2, g_done = sem("g_e2"), sem("g_done")
        xn_ready, o_psum, x1_ready = sem("xn_ready"), sem("o_psum"), sem("x1_ready")
        z2_ready, t2_psum, h2_ready = sem("z2_ready"), sem("t2_psum"), sem("h2_ready")
        cr_psum, sr_ready = sem("cr_psum"), sem("sr_ready")
        key_psum, silu_done = sem("key_psum"), sem("silu_done")
        inner_made = sem("inner_made")
        inner_hi, inner_lo = sem("inner_hi"), sem("inner_lo")
        value_psum, value_gated, x2_added = sem("value_psum"), sem("value_gated"), sem("x2_added")
        z3_ready, t3_psum, z3_hi, z3_lo = sem("z3_ready"), sem("t3_psum"), sem("z3_hi"), sem("z3_lo")
        gate_psum, down_psum, x3_added = sem("gate_psum"), sem("down_psum"), sem("x3_added")
        out_stored = sem("out_stored")

        block = ctx.enter_context(nc.Block())

        @block.sync
        def _(sp):
            def load(item, source):
                if item >= STAGES:
                    sp.wait_ge(item_done, item - STAGES + 1)
                sp.dma_start(staging[:, item % STAGES, :], source).then_inc(staged[item % STAGES], 16)

            def load_x_again(b):
                sp.wait_ge(op_made, operand_at("v", b) + KT)
                sp.dma_start(feat[:, :, b, 1:1 + BT], x_blocks[b]).then_inc(x_again[b], 16)

            sp.dma_start(resid[:, 0], x_blocks[0]).then_inc(x_loaded[0], 16)
            sp.dma_start(vec[:], vectors).then_inc(vec_loaded, 16)
            sp.dma_start(ident[:], identity).then_inc(ident_loaded, 16)
            for item in range(ITEM_R, ITEM_R + STAGES):
                load(item, wts[piece(item)])
            for b in range(1, BLOCKS):
                sp.dma_start(resid[:, b], x_blocks[b]).then_inc(x_loaded[b], 16)
            for item in range(ITEM_R + STAGES, ITEM_X):
                load(item, wts[piece(item)])
            for b in range(BLOCKS):
                load_x_again(b)
            for b in range(BLOCKS):
                for s in range(SUBS):
                    load(ITEM_X + b * SUBS + s, x_blocks[b][:, s, :])
            with sp.Fori(0, (ITEMS - ITEM_CM) // STAGES) as i:
                for n in range(STAGES):
                    sp.wait_ge(item_done, STAGES * i + (ITEM_CM + n - STAGES + 1))
                    source = wts[bass.ds(STAGES * i + (piece(ITEM_CM) + n), 1)].rearrange("o p n -> (o p) n")
                    sp.dma_start(staging[:, n, :], source).then_inc(staged[n], 16)
            for b in range(BLOCKS):
                sp.wait_ge(x3_added, SUBS * (UNITS - BLOCKS + b + 1))
                sp.dma_start(out_blocks[b], resid[:, b]).then_inc(out_stored, 16)
            sp.wait_ge(out_stored, 16 * BLOCKS)

        @block.tensor
        def _(pe):
            def three_passes(acc, left, right, first, last):
                pe.matmul(acc, left(0), right(0), start=first, stop=False)
                pe.matmul(acc, left(0), right(1), start=False, stop=False)
                return pe.matmul(acc, left(1), right(0), start=False, stop=last)

            def features(kind, b, item, row, banks, done, bank_free):
                slot = slot_of(kind, b)
                for j in range(KT):
                    bank_free(j)
                    for k in range(KT):
                        if j == 0:
                            pe.wait_ge(item_done, item + k + 1)
                            pe.wait_ge(op_lo, operand_at(kind, b) + k + 1)
                        mm = three_passes(banks[j][:], lambda p: weights[:, row + k, p, j * P:(j + 1) * P],
                                          lambda p: operand[:, slot, k, p, :], k == 0, k == KT - 1)
                    mm.then_inc(done, 1)

            def tokens(kind, b, item, row, done, bank_free):
                slot = slot_of(kind, b)
                for s in range(SUBS):
                    bank_free(s)
                    for k in range(KT):
                        if s == 0:
                            pe.wait_ge(item_done, item + k + 1)
                            pe.wait_ge(op_lo, operand_at(kind, b) + k + 1)
                        mm = three_passes(B[s][:], lambda p: operand[:, slot, k, p, s * P:(s + 1) * P],
                                          lambda p: weights[:, row + k, p, :], k == 0, k == KT - 1)
                    mm.then_inc(done, 1)

            def transposes(source, banks, done, bank_free):
                for k in range(KT):
                    bank_free(k)
                    for s in range(SUBS):
                        mm = pe.transpose(banks[k][:, s * P:(s + 1) * P], source(s)[:, k * P:(k + 1) * P], ident[:])
                    mm.then_inc(done, 1)

            def norm1(b):
                def bank_free(k):
                    if b == 1:
                        pe.wait_ge(h1_ready, k + 1)
                    if b >= 2:
                        pe.wait_ge(g_done, KT * (b - 2) + k + 1)
                pe.wait_ge(z1_ready, SUBS * (b + 1))
                transposes(lambda s: resid[:, b, s, :], B, t1_psum, bank_free)

            def receptance(b):
                def bank_free(j):
                    if b:
                        pe.wait_ge(r_gate, KT * (b - 1) + j + 1)
                features("r", b, ITEM_R, ROW_R, A, r_psum, bank_free)

            def key(b):
                def bank_free(j):
                    if b < BLOCKS - 1:
                        pe.wait_ge(h1_ready, KT * (b + 1) + j + 1)
                    else:
                        pe.wait_ge(g_done, KT * (b - 1) + j + 1)
                features("k", b, ITEM_K, ROW_K, B, k_psum, bank_free)

            def value(b):
                def bank_free(j):
                    if b:
                        pe.wait_ge(op_made, operand_at("y", b - 1) + j + 1)
                    else:
                        pe.wait_ge(r_gate, KT * (BLOCKS - 1) + j + 1)
                features("v", b, ITEM_V, ROW_V, A, v_psum, bank_free)

            def output(b):
                def bank_free(s):
                    if b:
                        pe.wait_ge(x1_ready, SUBS * (b - 1) + s + 1)
                    else:
                        pe.wait_ge(g_done, KT * (BLOCKS - 1) + s + 1)
                tokens("y", b, ITEM_O, ROW_O, o_psum, bank_free)

            def norm2(b):
                def bank_free(k):
                    if b:
                        pe.wait_ge(h2_ready, KT * (b - 1) + k + 1)
                    else:
                        pe.wait_ge(op_made, operand_at("y", BLOCKS - 1) + k + 1)
                pe.wait_ge(z2_ready, SUBS * (b + 1))
                transposes(lambda s: token_tile(b, s), A, t2_psum, bank_free)

            def channel_receptance(b):
                def bank_free(s):
                    if b:
                        pe.wait_ge(sr_ready, SUBS * (b - 1) + s + 1)
                    else:
                        pe.wait_ge(x1_ready, SUBS * (BLOCKS - 1) + s + 1)
                tokens("cr", b, ITEM_CR, ROW_CR, cr_psum, bank_free)

            def group_features(acc, b, row, i):
                for k in range(KT):
                    r, c = row + k // 2, (k % 2) * GROUP * P + i * P
                    mm = three_passes(acc, lambda p: weights[:, r, p, c:c + P],
                                      lambda p: operand[:, b, k, p, :], k == 0, k == KT - 1)
                return mm

            def group_tokens(acc, u, s, row):
                for i in range(GROUP):
                    mm = three_passes(acc, lambda p: inner(u, i, p)[:, s * P:(s + 1) * P],
                                      lambda p: weights[:, row + i, p, :], i == 0, i == GROUP - 1)
                return mm

            def channel_key(v, turn, bank_free=None):
                g, b = v // BLOCKS, v % BLOCKS
                if b == 0:
                    pe.wait_ge(item_done, 2 * CM_PIECES * turn + (ITEM_CM + CM_PIECES * g + 2))
                if g == 0:
                    pe.wait_ge(op_lo, operand_at("ck", b) + KT)
                for i in range(GROUP):
                    if bank_free:
                        bank_free(i)
                    else:
                        pe.wait_ge(silu_done, GROUP * PAIR * turn + (GROUP * (v - 2) + i + 1))
                    group_features(A[(GROUP * v + i) % 4][:], b, row_cm(g), i).then_inc(key_psum, 1)

            def channel_value(v, turn):
                g, b = v // BLOCKS, v % BLOCKS
                if b == 0:
                    pe.wait_ge(item_done, 2 * CM_PIECES * turn + (ITEM_CM + CM_PIECES * (g + 1)))
                pe.wait_ge(inner_lo, GROUP * PAIR * turn + GROUP * (v + 1))
                for s in range(SUBS):
                    if v == 0:
                        pe.wait_ge(sr_ready, SUBS * (BLOCKS - 1) + s + 1)
                    else:
                        pe.wait_ge(x2_added, SUBS * PAIR * turn + (SUBS * (v - 1) + s + 1))
                    group_tokens(B[s][:], v, s, row_cm(g) + GROUP).then_inc(value_psum, 1)

            def norm3(b, bank_free):
                pe.wait_ge(z3_ready, SUBS * (b + 1))
                transposes(lambda s: token_tile(b, s), A, t3_psum, bank_free)

            def ffn_in(v, turn, after_norm3=None):
                g, b = v // BLOCKS, v % BLOCKS
                if b == 0:
                    pe.wait_ge(item_done, 2 * FFN_PIECES * turn + (ITEM_FFN + FFN_PIECES * g + 2 * GROUP))
                if g == 0:
                    pe.wait_ge(z3_lo, KT * (b + 1))
                for i in range(GROUP):
                    if after_norm3 is None:
                        pe.wait_ge(inner_made, GROUP * PAIR * turn + (GROUP * (v - 1) + i + 1))
                    else:
                        pe.wait_ge(z3_lo, KT * after_norm3 + 2 * i + 2)
                    group_features(A[2 * i][:], b, row_ffn(g), i)
                    group_features(A[2 * i + 1][:], b, row_ffn(g) + GROUP, i).then_inc(gate_psum, 1)

            def ffn_out(v, turn):
                g, b = v // BLOCKS, v % BLOCKS
                if b == 0:
                    pe.wait_ge(item_done, 2 * FFN_PIECES * turn + (ITEM_FFN + FFN_PIECES * (g + 1)))
                pe.wait_ge(inner_lo, GROUP * PAIR * turn + GROUP * (UNITS + v + 1))
                for s in range(SUBS):
                    if v == 0:
                        pe.wait_ge(x2_added, SUBS * (UNITS - 1) + s + 1)
                    else:
                        pe.wait_ge(x3_added, SUBS * PAIR * turn + (SUBS * (v - 1) + s + 1))
                    group_tokens(B[s][:], v, s, row_ffn(g) + 2 * GROUP).then_inc(down_psum, 1)

            pe.wait_ge(ident_loaded, 16)
            norm1(0)
            receptance(0)
            for b in range(1, BLOCKS):
                norm1(b)
                key(b - 1)
                receptance(b)
            key(BLOCKS - 1)
            for b in range(BLOCKS):
                value(b)
            output(0)
            for b in range(1, BLOCKS):
                output(b)
                norm2(b - 1)
            channel_receptance(0)
            norm2(BLOCKS - 1)
            for b in range(1, BLOCKS):
                channel_receptance(b)
            for v in range(2):
                channel_key(v, 0, lambda i: pe.wait_ge(h2_ready, KT * BLOCKS))
            channel_value(0, 0)
            with pe.Fori(0, TURNS) as turn:
                for v in range(1, PAIR + 1):
                    channel_key(v + 1, turn)
                    channel_value(v, turn)
            for v in range(UNITS - PAIR + 1, UNITS - 2):
                channel_key(v + 1, 0)
                channel_value(v, 0)
            norm3(0, lambda k: pe.wait_ge(silu_done, GROUP * (UNITS - 2) + k + 1 if k < 2
                                          else GROUP * (UNITS - 3) + k - 1))
            channel_key(UNITS - 1, 0, lambda i: pe.wait_ge(z3_lo, 2 + i + 1))
            channel_value(UNITS - 2, 0)
            norm3(1, lambda k: pe.wait_ge(z3_lo, k + 1) if k < 2
                  else pe.wait_ge(silu_done, GROUP * (UNITS - 1) + k - 1))
            ffn_in(0, 0, after_norm3=1)
            channel_value(UNITS - 1, 0)
            norm3(2, lambda k: pe.wait_ge(inner_made, k // 2 + 1))
            ffn_in(1, 0, after_norm3=2)
            ffn_out(0, 0)
            norm3(3, lambda k: pe.wait_ge(inner_made, GROUP + k // 2 + 1))
            pe.wait_ge(z3_lo, KT * BLOCKS)
            with pe.Fori(0, TURNS) as turn:
                for v in range(2, PAIR + 2):
                    ffn_in(v, turn)
                    ffn_out(v - 1, turn)
            for v in range(UNITS - PAIR + 2, UNITS):
                ffn_in(v, 0)
                ffn_out(v - 1, 0)
            ffn_out(UNITS - 1, 0)

        @block.scalar
        def _(act):
            def weight_hi(item, row, parity):
                act.wait_ge(staged[parity], 8 * (item - parity) + 16)
                act.activation(weights[:, row, 0, :], staging[:, parity, :], ACT.Copy).then_inc(w_hi, 1)

            def matrix_hi(item, row):
                for k in range(KT):
                    weight_hi(item + k, row + k, (item + k) % STAGES)

            def operand_hi(kind, b, slot_free):
                n = operand_at(kind, b)
                for k in range(KT):
                    act.wait_ge(op_made, n + k + 1)
                    if k == 0:
                        slot_free()
                    act.activation(operand[:, slot_of(kind, b), k, 0, :], made[:, (n + k) % RING, :],
                                   ACT.Copy).then_inc(op_hi, 1)

            def norm1(b):
                for k in range(KT):
                    act.wait_ge(t1_psum, KT * b + k + 1)
                    act.activation(feat[:, k, b, 1:1 + BT], B[k][:], ACT.Identity, bias=vec[:, 1, k:k + 1],
                                   scale=vec[:, 0, k:k + 1]).then_inc(h1_ready, 1)

            def receptance_gate(b):
                for j in range(KT):
                    act.wait_ge(r_psum, KT * b + j + 1)
                    act.activation(resid[:, b, j, :], A[j][:], ACT.Sigmoid).then_inc(r_gate, 1)

            def wkv_weight(b):
                for j in range(KT):
                    act.wait_ge(k_low, KT * b + j + 1)
                    if b or j:
                        act.wait_ge(g_e2, KT * b + j)
                    act.activation(e2[:], B[j][:], ACT.Exp).then_inc(e2_ready, 1)
                    act.activation(B[j][:], B[j][:], ACT.Exp, scale=-1.0).then_inc(e2_inv, 1)

            def mix_hi(kind, b):
                def slot_free():
                    if kind == "r" and b >= 2:
                        act.wait_ge(r_psum, KT * (b - 1))
                    if kind == "k" and b >= 2:
                        act.wait_ge(k_psum, KT * (b - 1))
                    if kind == "v":
                        act.wait_ge(k_psum if b % 2 else r_psum, KT * (3 + b // 2))
                    if kind == "y":
                        act.wait_ge(v_psum, KT * (b + 1))
                    if kind == "cr":
                        act.wait_ge(o_psum, SUBS * (b + 1))
                    if kind == "ck":
                        act.wait_ge(cr_psum, SUBS * (b + 1))
                operand_hi(kind, b, slot_free)

            def norm2(b):
                act.wait_ge(t2_psum, KT * (b + 1))
                for k in range(KT):
                    act.activation(feat[:, k, b, 1:1 + BT], A[k][:], ACT.Identity, bias=vec[:, 3, k:k + 1],
                                   scale=vec[:, 2, k:k + 1]).then_inc(h2_ready, 1)

            def channel_receptance(b):
                act.wait_ge(op_made, operand_at("ck", b) + KT)
                if b < BLOCKS - 1:
                    act.wait_ge(edge_ready, BLOCKS - 1 + b + 1)
                for s in range(SUBS):
                    act.wait_ge(cr_psum, SUBS * b + s + 1)
                    act.activation(token_tile(b, s), B[s][:], ACT.Sigmoid).then_inc(sr_ready, 1)

            def inner_hi_tile(v, i):
                q = GROUP * v + i
                act.activation(inner(v, i, 0), made[:, q % RING, :], ACT.Copy).then_inc(inner_hi, 1)

            def channel_unit(v, turn):
                tiles = GROUP * PAIR * turn
                for i in range(GROUP):
                    q = GROUP * v + i
                    act.wait_ge(key_psum, tiles + (q + 1))
                    if v < 2:
                        act.wait_ge(op_lo, OPERANDS - RING + q + 1)
                    else:
                        act.wait_ge(inner_lo, tiles + (q - RING + 1))
                    act.activation(made[:, q % RING, :], A[q % 4][:], ACT.Silu).then_inc(silu_done, 1)
                if v < 2:
                    act.wait_ge(o_psum, SUBS * BLOCKS)
                else:
                    act.wait_ge(value_psum, SUBS * PAIR * turn + SUBS * (v - 1))
                for i in range(GROUP):
                    act.wait_ge(silu_done, tiles + (GROUP * v + i + 1))
                    inner_hi_tile(v, i)

            def channel_piece(v, turn):
                g, n = v // BLOCKS + 1, v % BLOCKS
                item = ITEM_CM + CM_PIECES * g + n
                if g == 1:
                    act.wait_ge(v_psum, KT * BLOCKS)
                if g >= 2:
                    if n < 2:
                        act.wait_ge(key_psum, GROUP * PAIR * turn + GROUP * BLOCKS * (g - 1))
                    else:
                        act.wait_ge(value_psum, SUBS * PAIR * turn + SUBS * BLOCKS * (g - 1))
                weight_hi(2 * CM_PIECES * turn + item, row_cm(g) + n, item % STAGES)

            SHARES = [(0, 1), (2, 3), (4,), (5,)]

            def first_ffn_piece(n):
                if n < 2 * GROUP:
                    act.wait_ge(cr_psum, SUBS * BLOCKS)
                else:
                    act.wait_ge(key_psum, GROUP * BLOCKS * (GROUPS - 1))
                weight_hi(ITEM_FFN + n, row_ffn(0) + n, (ITEM_FFN + n) % STAGES)

            def ffn_pieces(v, turn):
                g, b = v // BLOCKS + 1, v % BLOCKS
                for n in SHARES[b]:
                    item = ITEM_FFN + FFN_PIECES * g + n
                    if g == 1:
                        if n < 2:
                            act.wait_ge(value_psum, SUBS * BLOCKS * (GROUPS - 1))
                        elif n < 4:
                            act.wait_ge(key_psum, GROUP * UNITS)
                        else:
                            act.wait_ge(value_psum, SUBS * UNITS)
                    if g >= 2:
                        if n < 2 * GROUP:
                            act.wait_ge(gate_psum, GROUP * PAIR * turn + GROUP * BLOCKS * (g - 1))
                        else:
                            act.wait_ge(down_psum, SUBS * PAIR * turn + SUBS * BLOCKS * (g - 1))
                    weight_hi(2 * FFN_PIECES * turn + item, row_ffn(g) + n, item % STAGES)

            def norm3(b):
                act.wait_ge(key_psum, GROUP * (UNITS - BLOCKS + b + 1))
                for k in range(KT):
                    act.wait_ge(t3_psum, KT * b + k + 1)
                    act.activation(operand[:, b, k, 0, :], A[k][:], ACT.Copy).then_inc(z3_hi, 1)

            def ffn_unit(v, turn):
                tiles = GROUP * PAIR * turn
                for i in range(GROUP):
                    q = GROUP * v + i
                    act.wait_ge(gate_psum, tiles + (q + 1))
                    act.wait_ge(inner_lo, tiles + (GROUP * UNITS + q - RING + 1))
                    act.activation(made[:, q % RING, :], A[2 * i][:], ACT.Silu).then_inc(silu_done, 1)
                if v < 2:
                    act.wait_ge(value_psum, SUBS * (UNITS + v - 1))
                else:
                    act.wait_ge(down_psum, SUBS * PAIR * turn + SUBS * (v - 1))
                for i in range(GROUP):
                    act.wait_ge(inner_made, tiles + (GROUP * v + i + 1))
                    inner_hi_tile(v, i)

            act.wait_ge(vec_loaded, 16)
            matrix_hi(ITEM_R, ROW_R)
            norm1(0)
            mix_hi("r", 0)
            matrix_hi(ITEM_K, ROW_K)
            mix_hi("k", 0)
            for b in range(1, BLOCKS):
                receptance_gate(b - 1)
                norm1(b)
                mix_hi("r", b)
                if b < 3:
                    matrix_hi((ITEM_V, ITEM_O)[b - 1], (ROW_V, ROW_O)[b - 1])
                wkv_weight(b - 1)
                mix_hi("k", b)
            receptance_gate(BLOCKS - 1)
            mix_hi("v", 0)
            mix_hi("v", 1)
            wkv_weight(BLOCKS - 1)
            mix_hi("v", 2)
            mix_hi("v", 3)
            act.wait_ge(r_psum, KT * BLOCKS)
            matrix_hi(ITEM_CR, ROW_CR)
            for b in range(BLOCKS):
                mix_hi("y", b)
            for b in range(3):
                norm2(b)
                mix_hi("cr", b)
            mix_hi("ck", 0)
            channel_receptance(0)
            norm2(3)
            mix_hi("cr", 3)
            channel_receptance(1)
            mix_hi("ck", 1)
            act.wait_ge(k_psum, KT * BLOCKS)
            matrix_hi(ITEM_CM, row_cm(0))
            channel_receptance(2)
            mix_hi("ck", 2)
            channel_receptance(3)
            mix_hi("ck", 3)
            for v in range(BLOCKS):
                channel_unit(v, 0)
                channel_piece(v, 0)
            with act.Fori(0, TURNS) as turn:
                for v in range(BLOCKS, PAIR + BLOCKS):
                    channel_unit(v, turn)
                    channel_piece(v, turn)
            for v in range(UNITS - BLOCKS, UNITS - 1):
                channel_unit(v, 0)
                for n in SHARES[v % BLOCKS]:
                    first_ffn_piece(n)
            norm3(0)
            channel_unit(UNITS - 1, 0)
            for n in SHARES[3]:
                first_ffn_piece(n)
            norm3(1)
            for v in range(BLOCKS):
                ffn_unit(v, 0)
                ffn_pieces(v, 0)
                if v < 2:
                    norm3(2 + v)
            with act.Fori(0, TURNS) as turn:
                for v in range(BLOCKS, PAIR + BLOCKS):
                    ffn_unit(v, turn)
                    ffn_pieces(v, turn)
            for v in range(UNITS - BLOCKS, UNITS):
                ffn_unit(v, 0)

        @block.vector
        def _(dve):
            edges = [0]

            def first_token():
                dve.memset(feat[:, :, 0, 0:1], 0.0).then_inc(const_done, 1)

            def constants():
                dve.wait_ge(vec_loaded, 16)
                dve.tensor_scalar(rest[:], vec[:, 5:10, :], -1.0, 1.0, ALU.mult, ALU.add).then_inc(const_done, 1)
                dve.tensor_scalar(bonus[:], vec[:, 4, :], NO_STATE, None, ALU.add).then_inc(const_done, 1)

            def norm_stats(n, tile_of, stats):
                for s in range(SUBS):
                    dve.bn_stats(moments[:, s, :], tile_of(s)).then_inc(ln_moments, 1)
                for s in range(SUBS):
                    dve.wait_ge(ln_moments, SUBS * n + s + 1)
                    dve.bn_aggr(stats[:, s, :], moments[:, s, :]).then_inc(ln_stats, 1)
                dve.wait_ge(ln_stats, SUBS * (n + 1))
                dve.tensor_scalar(var_eps[:], stats[:, :, 1], EPS, None, ALU.add).then_inc(ln_var, 1)

            def norm1_stats(b):
                dve.wait_ge(x_loaded[b], 16)
                norm_stats(b, lambda s: resid[:, b, s, :], stats1[:, b])

            def norm1(b):
                dve.wait_ge(ln_rstd, b + 1)
                for s in range(SUBS):
                    dve.tensor_scalar(resid[:, b, s, :], resid[:, b, s, :], stats1[:, b, s, 0:1],
                                      rstd_both[:, s:s + 1], ALU.subtract, ALU.mult).then_inc(z1_ready, 1)

            def edge(b, ready):
                dve.wait_ge(ready, KT * b)
                dve.tensor_copy(feat[:, :, b, 0:1], feat[:, :, b - 1, BT:BT + 1]).then_inc(edge_ready, 1)
                edges[0] += 1

            def mix(kind, b, ready):
                n, m = operand_at(kind, b), MIXES[kind]
                parts = KT * [x for x in ORDER if x[0] != "y"].index((kind, b))
                if b:
                    dve.wait_ge(edge_ready, edges[0] if kind in ("r", "cr") else b)

                def rest_of(k):
                    dve.wait_ge(ready, KT * b + k + 1)
                    if n + k >= RING:
                        dve.wait_ge(op_lo, n + k - RING + 1)
                    dve.tensor_scalar(made[:, (n + k) % RING, :], feat[:, k, b, 0:BT], rest[:, m, k:k + 1], None,
                                      ALU.mult).then_inc(rest_part, 1)

                def whole(k):
                    dve.wait_ge(rest_part, parts + k + 1)
                    tile = made[:, (n + k) % RING, :]
                    dve.scalar_tensor_tensor(out=tile, in0=feat[:, k, b, 1:1 + BT], scalar=vec[:, 5 + m, k:k + 1],
                                             in1=tile, op0=ALU.mult, op1=ALU.add).then_inc(op_made, 1)

                rest_of(0)
                for k in range(1, KT):
                    rest_of(k)
                    whole(k - 1)
                whole(KT - 1)

            def wkv_weight(b):
                for j in range(KT):
                    dve.wait_ge(k_psum, KT * b + j + 1)
                    dve.tensor_scalar(B[j][:], B[j][:], bonus[:, j:j + 1], 0.0, ALU.add, ALU.min).then_inc(k_low, 1)
                for j in range(KT):
                    n = KT * b + j + 1
                    dve.wait_ge(r_gate, n)
                    dve.wait_ge(e2_ready, n)
                    dve.tensor_tensor(resid[:, b, j, :], resid[:, b, j, :], e2[:], ALU.mult).then_inc(g_e2, 1)
                    dve.wait_ge(g_e2, n)
                    dve.wait_ge(e2_inv, n)
                    dve.tensor_tensor(resid[:, b, j, :], B[j][:], resid[:, b, j, :], ALU.mult).then_inc(g_done, 1)

            def gated_value(b):
                n = operand_at("y", b)
                for j in range(KT):
                    dve.wait_ge(v_psum, KT * b + j + 1)
                    dve.wait_ge(g_done, KT * b + j + 1)
                    dve.wait_ge(op_lo, n + j - RING + 1)
                    dve.tensor_tensor(made[:, (n + j) % RING, :], A[j][:], resid[:, b, j, :],
                                      ALU.mult).then_inc(op_made, 1)

            def x_normed(b):
                dve.wait_ge(x_again[b], 16)
                for s in range(SUBS):
                    dve.tensor_scalar(resid[:, b, s, :], token_tile(b, s), stats1[:, b, s, 0:1],
                                      rstd[:, b, s:s + 1], ALU.subtract, ALU.mult).then_inc(xn_ready, 1)

            def output(b):
                for s in range(SUBS):
                    dve.wait_ge(o_psum, SUBS * b + s + 1)
                    dve.wait_ge(xn_ready, SUBS * b + s + 1)
                    dve.tensor_tensor(resid[:, b, s, :], B[s][:], resid[:, b, s, :], ALU.add).then_inc(x1_ready, 1)
                dve.wait_ge(x1_ready, SUBS * (b + 1))
                norm_stats(BLOCKS + b, lambda s: resid[:, b, s, :], stats2)

            def norm2(b):
                dve.wait_ge(ln_rstd, BLOCKS + b + 1)
                for s in range(SUBS):
                    dve.tensor_scalar(token_tile(b, s), resid[:, b, s, :], stats2[:, s, 0:1], rstd2[:, s:s + 1],
                                      ALU.subtract, ALU.mult).then_inc(z2_ready, 1)

            def channel_value(v, turn):
                b, tiles = v % BLOCKS, SUBS * PAIR * turn

                def gate(s):
                    dve.wait_ge(value_psum, tiles + (SUBS * v + s + 1))
                    dve.tensor_tensor(B[s][:], B[s][:], token_tile(b, s), ALU.mult).then_inc(value_gated, 1)

                def add(s):
                    dve.wait_ge(value_gated, tiles + (SUBS * v + s + 1))
                    dve.tensor_tensor(resid[:, b, s, :], B[s][:], resid[:, b, s, :], ALU.add).then_inc(x2_added, 1)

                gate(0)
                for s in range(1, SUBS):
                    gate(s)
                    add(s - 1)
                add(SUBS - 1)

            def norm3_stats(b):
                dve.wait_ge(x2_added, SUBS * (UNITS - BLOCKS + b + 1))
                norm_stats(2 * BLOCKS + b, lambda s: resid[:, b, s, :], stats2)

            def norm3(b):
                dve.wait_ge(ln_rstd, 2 * BLOCKS + b + 1)
                for s in range(SUBS):
                    dve.tensor_scalar(token_tile(b, s), resid[:, b, s, :], stats2[:, s, 0:1], rstd2[:, s:s + 1],
                                      ALU.subtract, ALU.mult).then_inc(z3_ready, 1)

            def norm3_lo(b):
                for k in range(KT):
                    dve.wait_ge(z3_hi, KT * b + k + 1)
                    dve.tensor_tensor(operand[:, b, k, 1, :], A[k][:], operand[:, b, k, 0, :].bitcast(F32),
                                      ALU.subtract).then_inc(z3_lo, 1)

            def ffn_gated(v, turn):
                tiles = GROUP * PAIR * turn
                for i in range(GROUP):
                    q = GROUP * v + i
                    dve.wait_ge(silu_done, tiles + (GROUP * UNITS + q + 1))
                    tile = made[:, q % RING, :]
                    dve.tensor_tensor(tile, A[2 * i + 1][:], tile, ALU.mult).then_inc(inner_made, 1)

            def ffn_out(v, turn):
                b, tiles = v % BLOCKS, SUBS * PAIR * turn
                for s in range(SUBS):
                    dve.wait_ge(down_psum, tiles + (SUBS * v + s + 1))
                    dve.tensor_tensor(resid[:, b, s, :], B[s][:], resid[:, b, s, :], ALU.add).then_inc(x3_added, 1)

            first_token()
            norm1_stats(0)
            constants()
            norm1(0)
            dve.wait_ge(const_done, 3)
            mix("r", 0, h1_ready)
            norm1_stats(1)
            mix("k", 0, h1_ready)
            norm1(1)
            for b in range(1, BLOCKS):
                edge(b, h1_ready)
                mix("r", b, h1_ready)
                if b + 1 < BLOCKS:
                    norm1_stats(b + 1)
                wkv_weight(b - 1)
                if b + 1 < BLOCKS:
                    norm1(b + 1)
                mix("k", b, h1_ready)
            mix("v", 0, h1_ready)
            mix("v", 1, h1_ready)
            wkv_weight(BLOCKS - 1)
            mix("v", 2, h1_ready)
            mix("v", 3, h1_ready)
            for b in range(BLOCKS):
                gated_value(b)
            x_normed(0)
            output(0)
            x_normed(1)
            norm2(0)
            output(1)
            norm2(1)
            x_normed(2)
            mix("cr", 0, h2_ready)
            output(2)
            norm2(2)
            x_normed(3)
            edge(1, h2_ready)
            mix("cr", 1, h2_ready)
            output(3)
            norm2(3)
            edge(2, h2_ready)
            mix("cr", 2, h2_ready)
            mix("ck", 0, h2_ready)
            edge(3, h2_ready)
            mix("cr", 3, h2_ready)
            for b in range(1, BLOCKS):
                mix("ck", b, h2_ready)
            dve.wait_ge(item_done, ITEM_CM)
            dve.wait_ge(sr_ready, SUBS * BLOCKS)
            with dve.Fori(0, TURNS) as turn:
                for v in range(PAIR):
                    channel_value(v, turn)
            for v in range(UNITS - PAIR, UNITS - BLOCKS):
                channel_value(v, 0)
            channel_value(UNITS - 4, 0)
            norm3_stats(0)
            norm3(0)
            channel_value(UNITS - 3, 0)
            norm3_stats(1)
            norm3(1)
            norm3_lo(0)
            channel_value(UNITS - 2, 0)
            norm3_stats(2)
            norm3(2)
            norm3_lo(1)
            ffn_gated(0, 0)
            channel_value(UNITS - 1, 0)
            norm3_stats(3)
            norm3_lo(2)
            norm3(3)
            ffn_gated(1, 0)
            ffn_out(0, 0)
            norm3_lo(3)
            with dve.Fori(0, TURNS) as turn:
                for v in range(2, PAIR + 2):
                    ffn_gated(v, turn)
                    ffn_out(v - 1, turn)
            for v in range(UNITS - PAIR + 2, UNITS):
                ffn_gated(v, 0)
                ffn_out(v - 1, 0)
            ffn_out(UNITS - 1, 0)

        @block.gpsimd
        def _(pool):
            steps = [0]

            def weight_lo(row, parity):
                pool.tensor_tensor(weights[:, row, 1, :], staging[:, parity, :], weights[:, row, 0, :].bitcast(F32),
                                   ALU.subtract).then_inc(item_done, 1)

            def matrix_lo(item, row):
                for k in range(KT):
                    pool.wait_ge(w_hi, piece(item + k) + 1)
                    weight_lo(row + k, (item + k) % STAGES)

            def x_added(b):
                for s in range(SUBS):
                    item = ITEM_X + SUBS * b + s
                    pool.wait_ge(staged[item % STAGES], 16 * (item // STAGES + 1))
                    pool.wait_ge(z2_ready, SUBS * b + s + 1)
                    pool.tensor_tensor(resid[:, b, s, :], resid[:, b, s, :], staging[:, item % STAGES, :],
                                       ALU.add).then_inc(item_done, 1)

            def operand_lo(kind, b):
                n = operand_at(kind, b)
                for k in range(KT):
                    slot = slot_of(kind, b)
                    pool.wait_ge(op_hi, n + k + 1)
                    pool.tensor_tensor(operand[:, slot, k, 1, :], made[:, (n + k) % RING, :],
                                       operand[:, slot, k, 0, :].bitcast(F32), ALU.subtract).then_inc(op_lo, 1)

            def step(ins):
                steps[0] += 1
                ins.then_inc(ln_step, 1)
                pool.wait_ge(ln_step, steps[0])

            def norm1(b):
                r, var = rstd[:, b], stats1[:, b, :, 1]
                pool.wait_ge(ln_var, b + 1)
                if b:
                    pool.wait_ge(z1_ready, SUBS * b)
                step(pool.tensor_tensor(r, var_eps[:], minus_half[:], ALU.pow))
                step(pool.tensor_tensor(scratch[:, 0], var, r, ALU.mult))
                step(pool.tensor_tensor(scratch[:, 1], scratch[:, 0], r, ALU.mult))
                step(pool.tensor_tensor(scratch[:, 2], scratch[:, 1], eps[:], ALU.add))
                step(pool.tensor_tensor(scratch[:, 3], scratch[:, 2], minus_half[:], ALU.pow))
                pool.tensor_tensor(rstd_both[:], r, scratch[:, 3], ALU.mult).then_inc(ln_rstd, 1)

            def norm(n):
                pool.wait_ge(ln_var, n + 1)
                pool.tensor_tensor(rstd2[:], var_eps[:], minus_half[:], ALU.pow).then_inc(ln_rstd, 1)

            def inner_lo_tiles(v, turn):
                for i in range(GROUP):
                    q = GROUP * v + i
                    pool.wait_ge(inner_hi, GROUP * PAIR * turn + (q + 1))
                    pool.tensor_tensor(inner(v, i, 1), made[:, q % RING, :], inner(v, i, 0).bitcast(F32),
                                       ALU.subtract).then_inc(inner_lo, 1)

            def ffn_lo_tiles(v, turn):
                for i in range(GROUP):
                    q = GROUP * v + i
                    pool.wait_ge(inner_hi, GROUP * PAIR * turn + (GROUP * UNITS + q + 1))
                    pool.tensor_tensor(inner(v, i, 1), made[:, q % RING, :], inner(v, i, 0).bitcast(F32),
                                       ALU.subtract).then_inc(inner_lo, 1)

            def channel_piece(v, turn):
                g, n = v // BLOCKS + 1, v % BLOCKS
                item = ITEM_CM + CM_PIECES * g + n
                pool.wait_ge(w_hi, 2 * CM_PIECES * turn + (piece(item) + 1))
                weight_lo(row_cm(g) + n, item % STAGES)

            SHARES = [(0, 1), (2, 3), (4,), (5,)]

            def ffn_pieces(b, g, turn):
                for n in SHARES[b]:
                    item = ITEM_FFN + FFN_PIECES * g + n
                    pool.wait_ge(w_hi, 2 * FFN_PIECES * turn + (piece(item) + 1))
                    weight_lo(row_ffn(g) + n, item % STAGES)

            step(pool.memset(minus_half[:], -0.5))
            step(pool.memset(eps[:], EPS))
            matrix_lo(ITEM_R, ROW_R)
            norm1(0)
            operand_lo("r", 0)
            norm1(1)
            matrix_lo(ITEM_K, ROW_K)
            operand_lo("k", 0)
            for b in range(1, BLOCKS):
                operand_lo("r", b)
                if b + 1 < BLOCKS:
                    norm1(b + 1)
                if b < 3:
                    matrix_lo((ITEM_V, ITEM_O)[b - 1], (ROW_V, ROW_O)[b - 1])
                operand_lo("k", b)
            for b in range(BLOCKS):
                operand_lo("v", b)
            matrix_lo(ITEM_CR, ROW_CR)
            for b in range(BLOCKS):
                operand_lo("y", b)
            norm(BLOCKS)
            x_added(0)
            norm(BLOCKS + 1)
            x_added(1)
            operand_lo("cr", 0)
            norm(BLOCKS + 2)
            x_added(2)
            operand_lo("cr", 1)
            norm(BLOCKS + 3)
            x_added(3)
            operand_lo("cr", 2)
            operand_lo("ck", 0)
            operand_lo("cr", 3)
            operand_lo("ck", 1)
            matrix_lo(ITEM_CM, row_cm(0))
            operand_lo("ck", 2)
            operand_lo("ck", 3)
            for v in range(2):
                inner_lo_tiles(v, 0)
                channel_piece(v, 0)
            with pool.Fori(0, TURNS) as turn:
                for v in range(2, PAIR + 2):
                    inner_lo_tiles(v, turn)
                    channel_piece(v, turn)
            for v in range(UNITS - PAIR + 2, UNITS - BLOCKS):
                inner_lo_tiles(v, 0)
                channel_piece(v, 0)
            inner_lo_tiles(UNITS - 4, 0)
            ffn_pieces(0, 0, 0)
            inner_lo_tiles(UNITS - 3, 0)
            ffn_pieces(1, 0, 0)
            norm(2 * BLOCKS)
            inner_lo_tiles(UNITS - 2, 0)
            ffn_pieces(2, 0, 0)
            norm(2 * BLOCKS + 1)
            inner_lo_tiles(UNITS - 1, 0)
            ffn_pieces(3, 0, 0)
            norm(2 * BLOCKS + 2)
            ffn_lo_tiles(0, 0)
            ffn_pieces(0, 1, 0)
            norm(2 * BLOCKS + 3)
            ffn_lo_tiles(1, 0)
            ffn_pieces(1, 1, 0)
            with pool.Fori(0, TURNS) as turn:
                for v in range(2, PAIR + 2):
                    ffn_lo_tiles(v, turn)
                    ffn_pieces(v % BLOCKS, v // BLOCKS + 1, turn)
            for v in range(UNITS - PAIR + 2, UNITS):
                ffn_lo_tiles(v, 0)
                if v < UNITS - BLOCKS:
                    ffn_pieces(v % BLOCKS, v // BLOCKS + 1, 0)


def kernel(**inputs):
    import numpy as np
    import concourse.bacc as bacc
    from concourse.bass_utils import run_bass_kernel_spmd

    def take(name):
        return np.asarray(inputs["L0_" + name])

    def feature_pieces(w):
        wt = w.T.reshape(KT, P, w.shape[0])
        if w.shape[0] == H:
            return list(wt)
        return [np.concatenate([wt[k], wt[k + 1]], axis=1) for k in range(0, KT, 2)]

    def inner_pieces(w):
        return list(w.T.reshape(GROUP, P, H))

    pieces = []
    for name in ("Wr", "Wk", "Wv", "Wo", "Wcr"):
        pieces += feature_pieces(take("attn_" + name))
    width = GROUP * P
    w_key, w_value = take("attn_Wkey"), take("attn_Wval")
    w_gate_up, w_down = take("ffn_w_gate_up"), take("ffn_w_down")
    for g in range(GROUPS):
        cut = slice(g * width, (g + 1) * width)
        pieces += feature_pieces(w_key[cut]) + inner_pieces(w_value[:, cut])
    for g in range(GROUPS):
        cut, up = slice(g * width, (g + 1) * width), slice(INNER + g * width, INNER + (g + 1) * width)
        pieces += feature_pieces(w_gate_up[cut]) + feature_pieces(w_gate_up[up]) + inner_pieces(w_down[:, cut])
    vectors = np.stack([take("attn_" + name).reshape(KT, P) for name in VECTORS])

    arrays = {
        "x": np.ascontiguousarray(take("attn_x")),
        "wts": np.ascontiguousarray(np.stack(pieces)),
        "vectors": np.ascontiguousarray(vectors.transpose(2, 0, 1)),
        "identity": np.eye(P, dtype=np.float32),
    }
    nc = bacc.Bacc("TRN2", target_bir_lowering=False, num_devices=1)
    args = [nc.dram_tensor(name, a.shape, F32, kind="ExternalInput").ap() for name, a in arrays.items()]
    out = nc.dram_tensor("out", (1, TOKENS, H), F32, kind="ExternalOutput").ap()
    build(nc, *args, out)
    r = run_bass_kernel_spmd(nc, [arrays], core_ids=[0])
    return r.results[0]["out"]
```

```python
from contextlib import ExitStack

import concourse.bass as bass
from concourse import mybir

ALU = mybir.AluOpType
ACT = mybir.ActivationFunctionType
F32 = mybir.dt.float32
F32R = mybir.dt.float32r

P = 128
H = 512
INNER = 2048
TOKENS = 2048
KT = H // P
BT = 512
BLOCKS = TOKENS // BT
SUBS = BT // P
EPS = 1e-5
NO_STATE = 1e38

GROUP = 2
GROUPS = INNER // (GROUP * P)
UNITS = GROUPS * BLOCKS
PAIR = 2 * BLOCKS
TURNS = GROUPS // 2 - 1

MATRIX = KT
CM_PIECES = 2 * GROUP
FFN_PIECES = 3 * GROUP
ITEM_R, ITEM_K, ITEM_V, ITEM_O, ITEM_CR = (n * MATRIX for n in range(5))
ITEM_CM = 5 * MATRIX
ITEM_FFN = ITEM_CM + GROUPS * CM_PIECES
ITEMS = ITEM_FFN + GROUPS * FFN_PIECES
STAGES = 2
EARLY = ITEM_V

ROW_R, ROW_K, ROW_V, ROW_O, ROW_CR = 0, 4, 8, 12, 0
ROW_ACT = 12


def row_cm(group):
    return 4 + CM_PIECES * (group % 2)


def row_ffn(group):
    return FFN_PIECES * (group % 2)


ORDER = ([(m, b) for b in range(BLOCKS) for m in ("r", "k")]
         + [("v", 0), ("v", 1), ("y", 0), ("v", 2), ("y", 1), ("v", 3), ("y", 2), ("y", 3)]
         + [(m, b) for b in range(BLOCKS) for m in ("cr", "ck")])
OPERANDS = KT * len(ORDER)
RING = 4


def operand_at(kind, b):
    return KT * ORDER.index((kind, b))


def slot_of(kind, b):
    return {"r": 2 * b, "k": 2 * b + 1}.get(kind, b) % BLOCKS


VECTORS = ["ln1_g", "ln1_b", "ln2_g", "ln2_b", "tm_first", "tm_mr", "tm_mk", "tm_mv", "cm_mr", "cm_mk"]
MIXES = {"r": 0, "k": 1, "v": 2, "cr": 3, "ck": 4}


def build(nc, x, wts, vectors, identity, out):
    x_blocks = x.rearrange("o (b s p) h -> (o b) p s h", p=P, s=SUBS)
    out_blocks = out.rearrange("o (b s p) h -> (o b) p s h", p=P, s=SUBS)

    with ExitStack() as ctx:
        def sb(name, shape, dt=F32):
            return ctx.enter_context(nc.sbuf_tensor(name, shape, dt))

        def sem(name):
            return ctx.enter_context(nc.semaphore(name))

        operand = sb("operand", [P, BLOCKS, KT, 2, BT], F32R)
        weights = sb("weights", [P, 16, 2, 512], F32R)
        feat = sb("feat", [P, KT, BLOCKS, 1 + BT])
        resid = sb("resid", [P, BLOCKS, SUBS, H])
        made = sb("made", [P, RING, BT])
        e2 = sb("e2", [P, BT])
        staging = sb("staging", [P, STAGES, 512])
        ident = sb("ident", [P, P])
        vec = sb("vec", [P, len(VECTORS), KT])
        rest = sb("rest", [P, len(MIXES), KT])
        bonus = sb("bonus", [P, KT])
        moments = sb("moments", [P, SUBS, 6])
        stats1 = sb("stats1", [P, BLOCKS, SUBS, 2])
        stats2 = sb("stats2", [P, SUBS, 2])
        var_eps = sb("var_eps", [P, 2, SUBS])
        rstd1 = sb("rstd1", [P, BLOCKS, 2, SUBS])
        rstd2 = sb("rstd2", [P, SUBS])
        minus_half = sb("minus_half", [P, 2, SUBS])

        bank = [ctx.enter_context(nc.psum_tensor(f"bank{i}", [P, 512], F32)) for i in range(8)]
        A, B = bank[:4], bank[4:]

        def early(item):
            return feat[:, item % KT, 2 + item // KT, 1:1 + BT]

        def landing(item):
            return early(item) if item < EARLY else staging[:, item % STAGES, :]

        def token_tile(b, s):
            return feat[:, s, b, 1:1 + BT]

        def place(kind, b, k, part):
            if kind == "cr":
                return weights[:, (ROW_K, ROW_V)[b % 2] + k, part, :]
            return operand[:, slot_of(kind, b), k, part, :]

        def inner(u, i, part):
            return weights[:, ROW_ACT + GROUP * (u % 2) + i, part, :]

        def norm3_banks(b):
            return B if b == BLOCKS - 1 else A

        vec_loaded, ident_loaded = sem("vec_loaded"), sem("ident_loaded")
        x_first = [sem(f"x_first{s}") for s in range(SUBS)]
        x_loaded = [sem(f"x_loaded{b}") for b in range(1, BLOCKS)]
        early_loaded = [sem(f"early_loaded{n}") for n in range(EARLY)]
        x_again = [sem(f"x_again{b}") for b in range(BLOCKS)]
        x_onto = [sem(f"x_onto{b}") for b in range(BLOCKS)]
        staged = [sem(f"staged{n}") for n in range(STAGES)]
        w_hi = sem("w_hi")
        item_done = sem("item_done")
        const_done = sem("const_done")
        ln_moments, ln_stats, ln_var = sem("ln_moments"), sem("ln_stats"), sem("ln_var")
        ln_rstd, half_set = sem("ln_rstd"), sem("half_set")
        first_var, first_rstd = sem("first_var"), sem("first_rstd")
        z1_ready, t1_psum, h1_ready = sem("z1_ready"), sem("t1_psum"), sem("h1_ready")
        edge_ready = sem("edge_ready")
        rest_part = sem("rest_part")
        op_made, op_hi, op_lo = sem("op_made"), sem("op_hi"), sem("op_lo")
        r_psum, k_psum, v_psum = sem("r_psum"), sem("k_psum"), sem("v_psum")
        r_gate, k_low, e2_ready, e2_inv = sem("r_gate"), sem("k_low"), sem("e2_ready"), sem("e2_inv")
        g_e2, g_done = sem("g_e2"), sem("g_done")
        xn_ready, o_psum, x1_ready = sem("xn_ready"), sem("o_psum"), sem("x1_ready")
        z2_ready, t2_psum, h2_ready = sem("z2_ready"), sem("t2_psum"), sem("h2_ready")
        cr_psum, sr_ready = sem("cr_psum"), sem("sr_ready")
        key_psum, silu_done = sem("key_psum"), sem("silu_done")
        inner_made = sem("inner_made")
        inner_hi, inner_lo = sem("inner_hi"), sem("inner_lo")
        value_psum, value_gated, x2_added = sem("value_psum"), sem("value_gated"), sem("x2_added")
        z3_ready, t3_psum, z3_hi, z3_lo = sem("z3_ready"), sem("t3_psum"), sem("z3_hi"), sem("z3_lo")
        gate_psum, down_psum, x3_added = sem("gate_psum"), sem("down_psum"), sem("x3_added")
        out_stored = sem("out_stored")

        block = ctx.enter_context(nc.Block())

        @block.sync
        def _(sp):
            def load(item, source):
                if item >= EARLY + STAGES:
                    sp.wait_ge(item_done, item - STAGES + 1)
                sp.dma_start(staging[:, item % STAGES, :], source).then_inc(staged[item % STAGES], 16)

            def load_early(items):
                for item in items:
                    sp.dma_start(early(item), wts[item]).then_inc(early_loaded[item], 16)

            def load_x_again(b):
                sp.wait_ge(op_made, operand_at("v", b) + KT)
                sp.dma_start(feat[:, :, b, 1:1 + BT], x_blocks[b]).then_inc(x_again[b], 16)

            for n in range(SUBS):
                sp.dma_start(resid[:, 0, n], x_blocks[0][:, n, :]).then_inc(x_first[n], 16)
            sp.dma_start(vec[:], vectors).then_inc(vec_loaded, 16)
            sp.dma_start(ident[:], identity).then_inc(ident_loaded, 16)
            load_early(range(ITEM_R, ITEM_K))
            sp.dma_start(resid[:, 1], x_blocks[1]).then_inc(x_loaded[0], 16)
            load_early(range(ITEM_K, ITEM_V))
            for b in range(2, BLOCKS):
                sp.dma_start(resid[:, b], x_blocks[b]).then_inc(x_loaded[b - 1], 16)
            for item in range(ITEM_V, ITEM_CR + STAGES):
                load(item, wts[item])
            for b in range(BLOCKS - 1):
                load_x_again(b)
            for item in range(ITEM_CR + STAGES, ITEM_CM):
                load(item, wts[item])
            load_x_again(BLOCKS - 1)
            with sp.Fori(0, (ITEMS - ITEM_CM) // STAGES) as i:
                for n in range(STAGES):
                    sp.wait_ge(item_done, STAGES * i + (ITEM_CM + n - STAGES + 1))
                    source = wts[bass.ds(STAGES * i + (ITEM_CM + n), 1)].rearrange("o p n -> (o p) n")
                    sp.dma_start(staging[:, n, :], source).then_inc(staged[n], 16)
            for b in range(BLOCKS - 1):
                sp.wait_ge(x3_added, SUBS * (UNITS - BLOCKS + b + 1))
                sp.dma_start(out_blocks[b], resid[:, b]).then_inc(out_stored, 16)
            for s in range(SUBS):
                sp.wait_ge(x3_added, SUBS * (UNITS - 1) + s + 1)
                sp.dma_start(out_blocks[BLOCKS - 1][:, s, :], resid[:, BLOCKS - 1, s]).then_inc(out_stored, 16)
            sp.wait_ge(out_stored, 16 * (BLOCKS - 1 + SUBS))

        @block.tensor
        def _(pe):
            def three_passes(acc, left, right, first, last):
                pe.matmul(acc, left(0), right(0), start=first, stop=False)
                pe.matmul(acc, left(0), right(1), start=False, stop=False)
                return pe.matmul(acc, left(1), right(0), start=False, stop=last)

            def features(kind, b, item, row, banks, done, bank_free, by_operand, between=None):
                def weight(j, k, part):
                    return weights[:, row + k, part, j * P:(j + 1) * P]

                if by_operand:
                    for k in range(KT):
                        pe.wait_ge(item_done, item + k + 1)
                        pe.wait_ge(op_hi, operand_at(kind, b) + k + 1)
                        for j in range(KT):
                            if k == 0:
                                bank_free(j)
                            pe.matmul(banks[j][:], weight(j, k, 0), place(kind, b, k, 0), start=k == 0, stop=False)
                            pe.matmul(banks[j][:], weight(j, k, 1), place(kind, b, k, 0), start=False, stop=False)
                        pe.wait_ge(op_lo, operand_at(kind, b) + k + 1)
                        for j in range(KT):
                            mm = pe.matmul(banks[j][:], weight(j, k, 0), place(kind, b, k, 1), start=False,
                                           stop=k == KT - 1)
                            if k == KT - 1:
                                mm.then_inc(done, 1)
                        if between and k == 0:
                            between()
                else:
                    for j in range(KT):
                        bank_free(j)
                        for k in range(KT):
                            if j == 0:
                                pe.wait_ge(item_done, item + k + 1)
                                pe.wait_ge(op_lo, operand_at(kind, b) + k + 1)
                            mm = three_passes(banks[j][:], lambda p: weight(j, k, p),
                                              lambda p: place(kind, b, k, p), k == 0, k == KT - 1)
                        mm.then_inc(done, 1)

            def tokens(kind, b, item, row, done, bank_free):
                for s in range(SUBS):
                    bank_free(s)
                    for k in range(KT):
                        if s == 0:
                            pe.wait_ge(item_done, item + k + 1)
                            pe.wait_ge(op_lo, operand_at(kind, b) + k + 1)
                        mm = three_passes(B[s][:], lambda p: place(kind, b, k, p)[:, s * P:(s + 1) * P],
                                          lambda p: weights[:, row + k, p, :], k == 0, k == KT - 1)
                    mm.then_inc(done, 1)

            def transposes(source, banks, done, bank_free):
                for k in range(KT):
                    bank_free(k)
                    for s in range(SUBS):
                        mm = pe.transpose(banks[k][:, s * P:(s + 1) * P], source(s)[:, k * P:(k + 1) * P], ident[:])
                    mm.then_inc(done, 1)

            def first_norm1():
                for s in range(SUBS):
                    pe.wait_ge(z1_ready, s + 1)
                    for k in range(KT):
                        mm = pe.transpose(A[k][:, s * P:(s + 1) * P], resid[:, 0, s, k * P:(k + 1) * P], ident[:])
                        if s == SUBS - 1:
                            mm.then_inc(t1_psum, 1)

            def norm1(b):
                def bank_free(k):
                    pe.wait_ge(r_gate, KT * (b - 1) + k + 1)
                pe.wait_ge(z1_ready, SUBS * (b + 1))
                transposes(lambda s: resid[:, b, s, :], A, t1_psum, bank_free)

            def receptance(b):
                def bank_free(j):
                    pe.wait_ge(h1_ready, KT * b + j + 1)
                features("r", b, ITEM_R, ROW_R, A, r_psum, bank_free, True)

            def key(b, between=None):
                def bank_free(j):
                    if b:
                        pe.wait_ge(g_done, KT * (b - 1) + j + 1)
                features("k", b, ITEM_K, ROW_K, B, k_psum, bank_free, True, between)

            def value(b):
                def bank_free(j):
                    if b:
                        pe.wait_ge(op_made, operand_at("y", b - 1) + j + 1)
                    else:
                        pe.wait_ge(r_gate, KT * (BLOCKS - 1) + j + 1)
                features("v", b, ITEM_V, ROW_V, A, v_psum, bank_free, False)

            def output(b):
                def bank_free(s):
                    if b:
                        pe.wait_ge(x1_ready, SUBS * (b - 1) + s + 1)
                    else:
                        pe.wait_ge(g_done, KT * (BLOCKS - 1) + s + 1)
                tokens("y", b, ITEM_O, ROW_O, o_psum, bank_free)

            def norm2(b):
                def bank_free(k):
                    if b:
                        pe.wait_ge(h2_ready, KT * (b - 1) + k + 1)
                    else:
                        pe.wait_ge(op_made, operand_at("y", BLOCKS - 1) + k + 1)
                pe.wait_ge(z2_ready, SUBS * (b + 1))
                transposes(lambda s: token_tile(b, s), A, t2_psum, bank_free)

            def channel_receptance(b):
                def bank_free(s):
                    if b:
                        pe.wait_ge(sr_ready, SUBS * (b - 1) + s + 1)
                    else:
                        pe.wait_ge(x1_ready, SUBS * (BLOCKS - 1) + s + 1)
                tokens("cr", b, ITEM_CR, ROW_CR, cr_psum, bank_free)

            def group_features(acc, b, row, i):
                for k in range(KT):
                    r, c = row + k // 2, (k % 2) * GROUP * P + i * P
                    mm = three_passes(acc, lambda p: weights[:, r, p, c:c + P],
                                      lambda p: operand[:, b, k, p, :], k == 0, k == KT - 1)
                return mm

            def group_tokens(acc, u, s, row):
                for i in range(GROUP):
                    mm = three_passes(acc, lambda p: inner(u, i, p)[:, s * P:(s + 1) * P],
                                      lambda p: weights[:, row + i, p, :], i == 0, i == GROUP - 1)
                return mm

            def channel_key(v, turn, bank_free=None):
                g, b = v // BLOCKS, v % BLOCKS
                if b == 0:
                    pe.wait_ge(item_done, 2 * CM_PIECES * turn + (ITEM_CM + CM_PIECES * g + 2))
                if g == 0:
                    pe.wait_ge(op_lo, operand_at("ck", b) + KT)
                for i in range(GROUP):
                    if bank_free:
                        bank_free(i)
                    else:
                        pe.wait_ge(silu_done, GROUP * PAIR * turn + (GROUP * (v - 2) + i + 1))
                    group_features(A[(GROUP * v + i) % 4][:], b, row_cm(g), i).then_inc(key_psum, 1)

            def channel_value(v, turn):
                g, b = v // BLOCKS, v % BLOCKS
                if b == 0:
                    pe.wait_ge(item_done, 2 * CM_PIECES * turn + (ITEM_CM + CM_PIECES * (g + 1)))
                pe.wait_ge(inner_lo, GROUP * PAIR * turn + GROUP * (v + 1))
                for s in range(SUBS):
                    if v == 0:
                        pe.wait_ge(sr_ready, SUBS * (BLOCKS - 1) + s + 1)
                    else:
                        pe.wait_ge(x2_added, SUBS * PAIR * turn + (SUBS * (v - 1) + s + 1))
                    group_tokens(B[s][:], v, s, row_cm(g) + GROUP).then_inc(value_psum, 1)

            def norm3(b, bank_free):
                pe.wait_ge(z3_ready, SUBS * (b + 1))
                transposes(lambda s: token_tile(b, s), norm3_banks(b), t3_psum, bank_free)

            def ffn_in(v, turn, after_norm3=None):
                g, b = v // BLOCKS, v % BLOCKS
                if b == 0:
                    pe.wait_ge(item_done, 2 * FFN_PIECES * turn + (ITEM_FFN + FFN_PIECES * g + 2 * GROUP))
                if g == 0:
                    pe.wait_ge(z3_lo, KT * (b + 1))
                for i in range(GROUP):
                    if after_norm3 is None:
                        pe.wait_ge(inner_made, GROUP * PAIR * turn + (GROUP * (v - 1) + i + 1))
                    else:
                        pe.wait_ge(z3_lo, KT * after_norm3 + 2 * i + 2)
                    group_features(A[2 * i][:], b, row_ffn(g), i)
                    group_features(A[2 * i + 1][:], b, row_ffn(g) + GROUP, i).then_inc(gate_psum, 1)

            def ffn_out(v, turn):
                g, b = v // BLOCKS, v % BLOCKS
                if b == 0:
                    pe.wait_ge(item_done, 2 * FFN_PIECES * turn + (ITEM_FFN + FFN_PIECES * (g + 1)))
                pe.wait_ge(inner_lo, GROUP * PAIR * turn + GROUP * (UNITS + v + 1))
                for s in range(SUBS):
                    if v == 0:
                        pe.wait_ge(x2_added, SUBS * (UNITS - 1) + s + 1)
                    else:
                        pe.wait_ge(x3_added, SUBS * PAIR * turn + (SUBS * (v - 1) + s + 1))
                    group_tokens(B[s][:], v, s, row_ffn(g) + 2 * GROUP).then_inc(down_psum, 1)

            pe.wait_ge(ident_loaded, 16)
            first_norm1()
            receptance(0)
            for b in range(BLOCKS - 1):
                key(b, lambda: norm1(b + 1))
                receptance(b + 1)
            key(BLOCKS - 1)
            for b in range(BLOCKS - 1):
                value(b)
            output(0)
            value(BLOCKS - 1)
            output(1)
            norm2(0)
            output(2)
            norm2(1)
            output(3)
            channel_receptance(0)
            norm2(2)
            channel_receptance(1)
            norm2(3)
            channel_receptance(2)
            channel_receptance(3)
            for v in range(2):
                channel_key(v, 0, lambda i: pe.wait_ge(h2_ready, KT * BLOCKS))
            channel_value(0, 0)
            with pe.Fori(0, TURNS) as turn:
                for v in range(1, PAIR + 1):
                    channel_key(v + 1, turn)
                    channel_value(v, turn)
            for v in range(UNITS - PAIR + 1, UNITS - 2):
                channel_key(v + 1, 0)
                channel_value(v, 0)
            channel_key(UNITS - 1, 0)
            norm3(0, lambda k: pe.wait_ge(silu_done, GROUP * (UNITS - 2) + k + 1))
            channel_value(UNITS - 2, 0)
            norm3(1, lambda k: pe.wait_ge(z3_lo, k + 1))
            channel_value(UNITS - 1, 0)
            ffn_in(0, 0, after_norm3=1)
            ffn_in(1, 0)
            ffn_out(0, 0)
            norm3(2, lambda k: pe.wait_ge(inner_made, GROUP + k // 2 + 1))
            ffn_out(1, 0)
            norm3(3, lambda k: pe.wait_ge(x3_added, SUBS + k + 1))
            ffn_in(2, 0, after_norm3=2)
            ffn_in(3, 0)
            ffn_out(2, 0)
            with pe.Fori(0, TURNS) as turn:
                for v in range(BLOCKS, PAIR + BLOCKS):
                    ffn_in(v, turn)
                    ffn_out(v - 1, turn)
            for v in range(UNITS - BLOCKS, UNITS):
                ffn_in(v, 0)
                ffn_out(v - 1, 0)
            ffn_out(UNITS - 1, 0)

        @block.scalar
        def _(act):
            def weight_hi(item, row, parity):
                act.wait_ge(staged[parity], 8 * (item - parity) + (16 - 8 * EARLY))
                act.activation(weights[:, row, 0, :], staging[:, parity, :], ACT.Copy).then_inc(w_hi, 1)

            def early_hi(item, row):
                for k in range(KT):
                    act.wait_ge(early_loaded[item + k], 16)
                    act.activation(weights[:, row + k, 0, :], early(item + k), ACT.Copy).then_inc(w_hi, 1)

            def matrix_hi(item, row, rows=range(KT)):
                for k in rows:
                    weight_hi(item + k, row + k, (item + k) % STAGES)

            def operand_hi(kind, b, k):
                n = operand_at(kind, b) + k
                act.wait_ge(op_made, n + 1)
                act.activation(place(kind, b, k, 0), made[:, n % RING, :], ACT.Copy).then_inc(op_hi, 1)

            def norm1_tile(b, k):
                act.wait_ge(t1_psum, KT * b + k + 1)
                act.activation(feat[:, k, b, 1:1 + BT], A[k][:], ACT.Identity, bias=vec[:, 1, k:k + 1],
                               scale=vec[:, 0, k:k + 1]).then_inc(h1_ready, 1)

            def norm1(b):
                if b == 2:
                    act.wait_ge(item_done, EARLY)
                for k in range(KT):
                    norm1_tile(b, k)

            def first_mix():
                for k in range(KT + 2):
                    if k >= 2:
                        operand_hi("r", 0, k - 2)
                    if k < KT:
                        norm1_tile(0, k)

            def receptance_gate(b):
                for j in range(KT):
                    act.wait_ge(r_psum, KT * b + j + 1)
                    act.activation(resid[:, b, j, :], A[j][:], ACT.Sigmoid).then_inc(r_gate, 1)

            def wkv_weight(b):
                for j in range(KT):
                    act.wait_ge(k_low, KT * b + j + 1)
                    if b or j:
                        act.wait_ge(g_e2, KT * b + j)
                    act.activation(e2[:], B[j][:], ACT.Exp).then_inc(e2_ready, 1)
                    act.activation(B[j][:], B[j][:], ACT.Exp, scale=-1.0).then_inc(e2_inv, 1)

            def mix_hi(kind, b, tiles=range(KT)):
                if kind == "r" and b >= 2:
                    act.wait_ge(r_psum, KT * (b - 1))
                if kind == "k" and b >= 2:
                    act.wait_ge(k_psum, KT * (b - 1))
                if kind == "v":
                    act.wait_ge(k_psum if b % 2 else r_psum, KT * (3 + b // 2))
                if kind == "y":
                    act.wait_ge(v_psum, KT * (b + 1))
                if kind == "cr" and b < 2:
                    act.wait_ge((k_psum, v_psum)[b], KT * BLOCKS)
                if kind == "cr" and b >= 2:
                    act.wait_ge(cr_psum, SUBS * (b - 1))
                if kind == "ck":
                    act.wait_ge(o_psum, SUBS * (b + 1))
                for k in tiles:
                    operand_hi(kind, b, k)

            def norm2(b):
                act.wait_ge(t2_psum, KT * (b + 1))
                for k in range(KT):
                    act.activation(feat[:, k, b, 1:1 + BT], A[k][:], ACT.Identity, bias=vec[:, 3, k:k + 1],
                                   scale=vec[:, 2, k:k + 1]).then_inc(h2_ready, 1)

            def channel_receptance(b):
                act.wait_ge(op_made, operand_at("ck", b) + KT)
                if b < BLOCKS - 1:
                    act.wait_ge(edge_ready, BLOCKS - 1 + b + 1)
                for s in range(SUBS):
                    act.wait_ge(cr_psum, SUBS * b + s + 1)
                    act.activation(token_tile(b, s), B[s][:], ACT.Sigmoid).then_inc(sr_ready, 1)

            def inner_hi_tile(v, i):
                q = GROUP * v + i
                act.activation(inner(v, i, 0), made[:, q % RING, :], ACT.Copy).then_inc(inner_hi, 1)

            def channel_unit(v, turn):
                tiles = GROUP * PAIR * turn
                for i in range(GROUP):
                    q = GROUP * v + i
                    act.wait_ge(key_psum, tiles + (q + 1))
                    if v < 2:
                        act.wait_ge(op_lo, OPERANDS - RING + q + 1)
                    else:
                        act.wait_ge(inner_lo, tiles + (q - RING + 1))
                    act.activation(made[:, q % RING, :], A[q % 4][:], ACT.Silu).then_inc(silu_done, 1)
                if v < 2:
                    act.wait_ge(o_psum, SUBS * BLOCKS)
                else:
                    act.wait_ge(value_psum, SUBS * PAIR * turn + SUBS * (v - 1))
                for i in range(GROUP):
                    act.wait_ge(silu_done, tiles + (GROUP * v + i + 1))
                    inner_hi_tile(v, i)

            def channel_piece(v, turn):
                g, n = v // BLOCKS + 1, v % BLOCKS
                item = ITEM_CM + CM_PIECES * g + n
                if g == 1:
                    act.wait_ge(cr_psum, SUBS * BLOCKS)
                if g >= 2:
                    if n < 2:
                        act.wait_ge(key_psum, GROUP * PAIR * turn + GROUP * BLOCKS * (g - 1))
                    else:
                        act.wait_ge(value_psum, SUBS * PAIR * turn + SUBS * BLOCKS * (g - 1))
                weight_hi(2 * CM_PIECES * turn + item, row_cm(g) + n, item % STAGES)

            SHARES = [(0, 1), (2, 3), (4,), (5,)]

            def first_ffn_piece(n):
                if n < 2 * GROUP:
                    act.wait_ge(cr_psum, SUBS * BLOCKS)
                else:
                    act.wait_ge(key_psum, GROUP * BLOCKS * (GROUPS - 1))
                weight_hi(ITEM_FFN + n, row_ffn(0) + n, (ITEM_FFN + n) % STAGES)

            def ffn_pieces(v, turn):
                g, b = v // BLOCKS + 1, v % BLOCKS
                for n in SHARES[b]:
                    item = ITEM_FFN + FFN_PIECES * g + n
                    if g == 1:
                        if n < 2:
                            act.wait_ge(value_psum, SUBS * BLOCKS * (GROUPS - 1))
                        elif n < 4:
                            act.wait_ge(key_psum, GROUP * UNITS)
                        else:
                            act.wait_ge(value_psum, SUBS * UNITS)
                    if g >= 2:
                        if n < 2 * GROUP:
                            act.wait_ge(gate_psum, GROUP * PAIR * turn + GROUP * BLOCKS * (g - 1))
                        else:
                            act.wait_ge(down_psum, SUBS * PAIR * turn + SUBS * BLOCKS * (g - 1))
                    weight_hi(2 * FFN_PIECES * turn + item, row_ffn(g) + n, item % STAGES)

            def norm3(b):
                act.wait_ge(key_psum, GROUP * (UNITS - BLOCKS + b + 1))
                for k in range(KT):
                    act.wait_ge(t3_psum, KT * b + k + 1)
                    act.activation(operand[:, b, k, 0, :], norm3_banks(b)[k][:], ACT.Copy).then_inc(z3_hi, 1)

            def ffn_unit(v, turn):
                tiles = GROUP * PAIR * turn
                for i in range(GROUP):
                    q = GROUP * v + i
                    act.wait_ge(gate_psum, tiles + (q + 1))
                    act.wait_ge(inner_lo, tiles + (GROUP * UNITS + q - RING + 1))
                    act.activation(made[:, q % RING, :], A[2 * i][:], ACT.Silu).then_inc(silu_done, 1)
                if v < 2:
                    act.wait_ge(value_psum, SUBS * (UNITS + v - 1))
                else:
                    act.wait_ge(down_psum, SUBS * PAIR * turn + SUBS * (v - 1))
                for i in range(GROUP):
                    act.wait_ge(inner_made, tiles + (GROUP * v + i + 1))
                    inner_hi_tile(v, i)

            act.wait_ge(vec_loaded, 16)
            early_hi(ITEM_R, ROW_R)
            first_mix()
            early_hi(ITEM_K, ROW_K)
            mix_hi("k", 0)
            receptance_gate(0)
            for b in range(1, BLOCKS):
                norm1(b)
                mix_hi("r", b)
                if b < 3:
                    matrix_hi((ITEM_V, ITEM_O)[b - 1], (ROW_V, ROW_O)[b - 1], range(2))
                mix_hi("k", b)
                wkv_weight(b - 1)
                receptance_gate(b)
                if b < 3:
                    matrix_hi((ITEM_V, ITEM_O)[b - 1], (ROW_V, ROW_O)[b - 1], range(2, KT))
            mix_hi("v", 0)
            mix_hi("v", 1)
            wkv_weight(BLOCKS - 1)
            for b in range(2):
                mix_hi("y", b)
                mix_hi("v", b + 2)
            matrix_hi(ITEM_CR, ROW_CR)
            mix_hi("y", 2)
            mix_hi("y", 3)
            norm2(0)
            mix_hi("cr", 0)
            norm2(1)
            mix_hi("ck", 0)
            mix_hi("cr", 1)
            mix_hi("ck", 1)
            channel_receptance(0)
            norm2(2)
            mix_hi("cr", 2)
            mix_hi("ck", 2, range(2))
            channel_receptance(1)
            mix_hi("ck", 2, range(2, KT))
            norm2(3)
            mix_hi("cr", 3)
            channel_receptance(2)
            matrix_hi(ITEM_CM, row_cm(0), range(GROUP))
            mix_hi("ck", 3)
            matrix_hi(ITEM_CM, row_cm(0), range(GROUP, CM_PIECES))
            channel_receptance(3)
            for v in range(BLOCKS):
                channel_unit(v, 0)
                channel_piece(v, 0)
            with act.Fori(0, TURNS) as turn:
                for v in range(BLOCKS, PAIR + BLOCKS):
                    channel_unit(v, turn)
                    channel_piece(v, turn)
            for v in range(UNITS - BLOCKS, UNITS - 1):
                channel_unit(v, 0)
                for n in SHARES[v % BLOCKS]:
                    first_ffn_piece(n)
            channel_unit(UNITS - 1, 0)
            for n in SHARES[3]:
                first_ffn_piece(n)
            norm3(0)
            norm3(1)
            for v in range(BLOCKS):
                ffn_unit(v, 0)
                ffn_pieces(v, 0)
                if v == 1:
                    norm3(2)
                    norm3(3)
            with act.Fori(0, TURNS) as turn:
                for v in range(BLOCKS, PAIR + BLOCKS):
                    ffn_unit(v, turn)
                    ffn_pieces(v, turn)
            for v in range(UNITS - BLOCKS, UNITS):
                ffn_unit(v, 0)

        @block.vector
        def _(dve):
            def first_token():
                dve.memset(feat[:, :, 0, 0:1], 0.0).then_inc(const_done, 1)

            def constants():
                dve.wait_ge(vec_loaded, 16)
                dve.tensor_scalar(rest[:], vec[:, 5:10, :], -1.0, 1.0, ALU.mult, ALU.add).then_inc(const_done, 1)
                dve.tensor_scalar(bonus[:], vec[:, 4, :], NO_STATE, None, ALU.add).then_inc(const_done, 1)

            def var_of_both(var, s, done):
                dve.tensor_scalar(var_eps[:, 0, s], var, EPS, None, ALU.add).then_inc(done, 1)
                dve.tensor_scalar(var_eps[:, 1, s], var, 1.0 + EPS, EPS * EPS, ALU.mult, ALU.add).then_inc(done, 1)

            def first_norm1():
                def normed(s):
                    dve.wait_ge(first_rstd, s + 1)
                    norm1_tile(0, s)

                def summed(s):
                    dve.wait_ge(x_first[s], 16)
                    dve.bn_stats(moments[:, s, :], resid[:, 0, s, :]).then_inc(ln_moments, 1)

                summed(0)
                for s in range(SUBS):
                    if s + 1 < SUBS:
                        summed(s + 1)
                    dve.wait_ge(ln_moments, s + 1)
                    dve.bn_aggr(stats1[:, 0, s, :], moments[:, s, :]).then_inc(ln_stats, 1)
                    dve.wait_ge(ln_stats, s + 1)
                    var_of_both(stats1[:, 0, s, 1:2], slice(s, s + 1), first_var)
                    if s:
                        normed(s - 1)
                normed(SUBS - 1)

            def norm_stats(n, tile_of, stats, again=False):
                for s in range(SUBS):
                    dve.bn_stats(moments[:, s, :], tile_of(s)).then_inc(ln_moments, 1)
                for s in range(SUBS):
                    dve.wait_ge(ln_moments, SUBS * n + s + 1)
                    dve.bn_aggr(stats[:, s, :], moments[:, s, :]).then_inc(ln_stats, 1)
                dve.wait_ge(ln_stats, SUBS * (n + 1))
                if again:
                    var_of_both(stats[:, :, 1], slice(None), ln_var)
                else:
                    dve.tensor_scalar(var_eps[:, 0], stats[:, :, 1], EPS, None, ALU.add).then_inc(ln_var, 1)

            def norm1_stats(b):
                dve.wait_ge(x_loaded[b - 1], 16)
                norm_stats(b, lambda s: resid[:, b, s, :], stats1[:, b], again=True)

            def norm1_tile(b, s):
                dve.tensor_scalar(resid[:, b, s, :], resid[:, b, s, :], stats1[:, b, s, 0:1],
                                  rstd1[:, b, 1, s:s + 1], ALU.subtract, ALU.mult).then_inc(z1_ready, 1)

            def norm1(b):
                dve.wait_ge(ln_rstd, b)
                for s in range(SUBS):
                    norm1_tile(b, s)

            def edge(b, ready):
                dve.wait_ge(ready, KT * b)
                dve.tensor_copy(feat[:, :, b, 0:1], feat[:, :, b - 1, BT:BT + 1]).then_inc(edge_ready, 1)

            def mix(kind, b, ready):
                n, m = operand_at(kind, b), MIXES[kind]
                parts = KT * [x for x in ORDER if x[0] != "y"].index((kind, b))
                if b:
                    dve.wait_ge(edge_ready, b if ready is h1_ready else BLOCKS - 1 + b)

                def rest_of(k):
                    dve.wait_ge(ready, KT * b + k + 1)
                    if n + k >= RING:
                        dve.wait_ge(op_lo, n + k - RING + 1)
                    dve.tensor_scalar(made[:, (n + k) % RING, :], feat[:, k, b, 0:BT], rest[:, m, k:k + 1], None,
                                      ALU.mult).then_inc(rest_part, 1)

                def whole(k):
                    dve.wait_ge(rest_part, parts + k + 1)
                    tile = made[:, (n + k) % RING, :]
                    dve.scalar_tensor_tensor(out=tile, in0=feat[:, k, b, 1:1 + BT], scalar=vec[:, 5 + m, k:k + 1],
                                             in1=tile, op0=ALU.mult, op1=ALU.add).then_inc(op_made, 1)

                if n == 0:
                    for k in range(KT):
                        rest_of(k)
                        whole(k)
                else:
                    rest_of(0)
                    for k in range(1, KT):
                        rest_of(k)
                        whole(k - 1)
                    whole(KT - 1)

            def wkv_low(b):
                for j in range(KT):
                    dve.wait_ge(k_psum, KT * b + j + 1)
                    dve.tensor_scalar(B[j][:], B[j][:], bonus[:, j:j + 1], 0.0, ALU.add, ALU.min).then_inc(k_low, 1)

            def wkv_weight(b):
                for j in range(KT):
                    n = KT * b + j + 1
                    dve.wait_ge(r_gate, n)
                    dve.wait_ge(e2_ready, n)
                    dve.tensor_tensor(resid[:, b, j, :], resid[:, b, j, :], e2[:], ALU.mult).then_inc(g_e2, 1)
                    dve.wait_ge(g_e2, n)
                    dve.wait_ge(e2_inv, n)
                    dve.tensor_tensor(resid[:, b, j, :], B[j][:], resid[:, b, j, :], ALU.mult).then_inc(g_done, 1)

            def gated_value(b):
                n = operand_at("y", b)
                for j in range(KT):
                    dve.wait_ge(v_psum, KT * b + j + 1)
                    dve.wait_ge(g_done, KT * b + j + 1)
                    dve.wait_ge(op_lo, n + j - RING + 1)
                    dve.tensor_tensor(made[:, (n + j) % RING, :], A[j][:], resid[:, b, j, :],
                                      ALU.mult).then_inc(op_made, 1)

            def x_normed(b):
                dve.wait_ge(x_again[b], 16)
                for s in range(SUBS):
                    dve.wait_ge(op_made, operand_at("y", b) + s + 1)
                    dve.tensor_scalar(resid[:, b, s, :], token_tile(b, s), stats1[:, b, s, 0:1],
                                      rstd1[:, b, 0, s:s + 1], ALU.subtract, ALU.mult).then_inc(xn_ready, 1)

            def output(b, tiles=range(SUBS)):
                for s in tiles:
                    dve.wait_ge(o_psum, SUBS * b + s + 1)
                    dve.wait_ge(xn_ready, SUBS * b + s + 1)
                    dve.tensor_tensor(resid[:, b, s, :], B[s][:], resid[:, b, s, :], ALU.add).then_inc(x1_ready, 1)

            def norm2_stats(b):
                dve.wait_ge(x1_ready, SUBS * (b + 1))
                norm_stats(BLOCKS + b, lambda s: resid[:, b, s, :], stats2)

            def norm2(b):
                dve.wait_ge(ln_rstd, BLOCKS + b)
                for s in range(SUBS):
                    dve.tensor_scalar(token_tile(b, s), resid[:, b, s, :], stats2[:, s, 0:1], rstd2[:, s:s + 1],
                                      ALU.subtract, ALU.mult).then_inc(z2_ready, 1)

            def channel_value(v, turn):
                b, tiles = v % BLOCKS, SUBS * PAIR * turn

                def gate(s):
                    dve.wait_ge(value_psum, tiles + (SUBS * v + s + 1))
                    dve.tensor_tensor(B[s][:], B[s][:], token_tile(b, s), ALU.mult).then_inc(value_gated, 1)

                def add(s):
                    dve.wait_ge(value_gated, tiles + (SUBS * v + s + 1))
                    dve.tensor_tensor(resid[:, b, s, :], B[s][:], resid[:, b, s, :], ALU.add).then_inc(x2_added, 1)

                gate(0)
                for s in range(1, SUBS):
                    gate(s)
                    add(s - 1)
                add(SUBS - 1)

            def norm3_stats(b):
                dve.wait_ge(x2_added, SUBS * (UNITS - BLOCKS + b + 1))
                norm_stats(2 * BLOCKS + b, lambda s: resid[:, b, s, :], stats2)

            def norm3(b):
                dve.wait_ge(ln_rstd, 2 * BLOCKS + b)
                for s in range(SUBS):
                    dve.tensor_scalar(token_tile(b, s), resid[:, b, s, :], stats2[:, s, 0:1], rstd2[:, s:s + 1],
                                      ALU.subtract, ALU.mult).then_inc(z3_ready, 1)

            def norm3_lo(b):
                for k in range(KT):
                    dve.wait_ge(z3_hi, KT * b + k + 1)
                    dve.tensor_tensor(operand[:, b, k, 1, :], norm3_banks(b)[k][:], operand[:, b, k, 0, :].bitcast(F32),
                                      ALU.subtract).then_inc(z3_lo, 1)

            def ffn_gated(v, turn, rows=range(GROUP)):
                tiles = GROUP * PAIR * turn
                for i in rows:
                    q = GROUP * v + i
                    dve.wait_ge(silu_done, tiles + (GROUP * UNITS + q + 1))
                    tile = made[:, q % RING, :]
                    dve.tensor_tensor(tile, A[2 * i + 1][:], tile, ALU.mult).then_inc(inner_made, 1)

            def ffn_out(v, turn):
                b, tiles = v % BLOCKS, SUBS * PAIR * turn
                for s in range(SUBS):
                    dve.wait_ge(down_psum, tiles + (SUBS * v + s + 1))
                    dve.tensor_tensor(resid[:, b, s, :], B[s][:], resid[:, b, s, :], ALU.add).then_inc(x3_added, 1)

            first_token()
            first_norm1()
            constants()
            dve.wait_ge(const_done, 3)
            mix("r", 0, h1_ready)
            norm1_stats(1)
            mix("k", 0, h1_ready)
            norm1(1)
            norm1_stats(2)
            for b in range(1, BLOCKS):
                edge(b, h1_ready)
                mix("r", b, h1_ready)
                if b + 1 < BLOCKS:
                    norm1(b + 1)
                mix("k", b, h1_ready)
                wkv_low(b - 1)
                wkv_weight(b - 1)
                if b + 2 < BLOCKS:
                    norm1_stats(b + 2)
            mix("v", 0, h1_ready)
            mix("v", 1, h1_ready)
            wkv_low(BLOCKS - 1)
            wkv_weight(BLOCKS - 1)
            gated_value(0)
            mix("v", 2, h1_ready)
            gated_value(1)
            mix("v", 3, h1_ready)
            x_normed(0)
            x_normed(1)
            gated_value(2)
            x_normed(2)
            output(0)
            norm2_stats(0)
            gated_value(3)
            norm2(0)
            x_normed(3)
            output(1)
            norm2_stats(1)
            mix("cr", 0, h2_ready)
            norm2(1)
            output(2)
            mix("ck", 0, h2_ready)
            edge(1, h2_ready)
            norm2_stats(2)
            output(3, range(2))
            mix("cr", 1, h2_ready)
            output(3, range(2, SUBS))
            norm2(2)
            mix("ck", 1, h2_ready)
            edge(2, h2_ready)
            norm2_stats(3)
            norm2(3)
            mix("cr", 2, h2_ready)
            mix("ck", 2, h2_ready)
            edge(3, h2_ready)
            mix("cr", 3, h2_ready)
            mix("ck", 3, h2_ready)
            for b in range(BLOCKS):
                dve.wait_ge(x_onto[b], 16)
            dve.wait_ge(sr_ready, SUBS * BLOCKS)
            with dve.Fori(0, TURNS) as turn:
                for v in range(PAIR):
                    channel_value(v, turn)
            for v in range(UNITS - PAIR, UNITS - BLOCKS):
                channel_value(v, 0)
            channel_value(UNITS - 4, 0)
            norm3_stats(0)
            norm3(0)
            channel_value(UNITS - 3, 0)
            norm3_stats(1)
            norm3_lo(0)
            norm3(1)
            channel_value(UNITS - 2, 0)
            norm3_lo(1)
            channel_value(UNITS - 1, 0)
            ffn_gated(0, 0, range(1))
            norm3_stats(2)
            ffn_gated(0, 0, range(1, GROUP))
            norm3(2)
            norm3_stats(3)
            norm3(3)
            ffn_gated(1, 0)
            ffn_out(0, 0)
            norm3_lo(2)
            ffn_out(1, 0)
            norm3_lo(3)
            ffn_gated(2, 0)
            ffn_gated(3, 0)
            ffn_out(2, 0)
            with dve.Fori(0, TURNS) as turn:
                for v in range(BLOCKS, PAIR + BLOCKS):
                    ffn_gated(v, turn)
                    ffn_out(v - 1, turn)
            for v in range(UNITS - BLOCKS, UNITS):
                ffn_gated(v, 0)
                ffn_out(v - 1, 0)
            ffn_out(UNITS - 1, 0)

        @block.gpsimd
        def _(pool):
            def weight_lo(row, raw):
                pool.tensor_tensor(weights[:, row, 1, :], raw, weights[:, row, 0, :].bitcast(F32),
                                   ALU.subtract).then_inc(item_done, 1)

            def matrix_lo(item, row, rows=range(KT)):
                for k in rows:
                    pool.wait_ge(w_hi, item + k + 1)
                    weight_lo(row + k, landing(item + k))

            def x_added(b):
                pool.wait_ge(z2_ready, SUBS * (b + 1))
                pool.dma_start(resid[:, b], x_blocks[b], accum_op=ALU.add).then_inc(x_onto[b], 16)

            def operand_lo(kind, b, tiles=range(KT)):
                n = operand_at(kind, b)
                for k in tiles:
                    pool.wait_ge(op_hi, n + k + 1)
                    pool.tensor_tensor(place(kind, b, k, 1), made[:, (n + k) % RING, :],
                                       place(kind, b, k, 0).bitcast(F32), ALU.subtract).then_inc(op_lo, 1)

            def first_norm1():
                for s in range(SUBS):
                    pool.wait_ge(first_var, 2 * (s + 1))
                    pool.tensor_tensor(rstd1[:, 0, :, s], var_eps[:, :, s], minus_half[:, :, s],
                                       ALU.pow).then_inc(first_rstd, 1)

            def norm1(b):
                pool.wait_ge(ln_var, 2 * b)
                pool.tensor_tensor(rstd1[:, b], var_eps[:], minus_half[:], ALU.pow).then_inc(ln_rstd, 1)

            def norm(n):
                pool.wait_ge(ln_var, BLOCKS + n - 1)
                pool.tensor_tensor(rstd2[:], var_eps[:, 0], minus_half[:, 0], ALU.pow).then_inc(ln_rstd, 1)

            def inner_lo_tiles(v, turn):
                for i in range(GROUP):
                    q = GROUP * v + i
                    pool.wait_ge(inner_hi, GROUP * PAIR * turn + (q + 1))
                    pool.tensor_tensor(inner(v, i, 1), made[:, q % RING, :], inner(v, i, 0).bitcast(F32),
                                       ALU.subtract).then_inc(inner_lo, 1)

            def ffn_lo_tiles(v, turn):
                for i in range(GROUP):
                    q = GROUP * v + i
                    pool.wait_ge(inner_hi, GROUP * PAIR * turn + (GROUP * UNITS + q + 1))
                    pool.tensor_tensor(inner(v, i, 1), made[:, q % RING, :], inner(v, i, 0).bitcast(F32),
                                       ALU.subtract).then_inc(inner_lo, 1)

            def channel_piece(v, turn):
                g, n = v // BLOCKS + 1, v % BLOCKS
                item = ITEM_CM + CM_PIECES * g + n
                pool.wait_ge(w_hi, 2 * CM_PIECES * turn + (item + 1))
                weight_lo(row_cm(g) + n, landing(item))

            SHARES = [(0, 1), (2, 3), (4,), (5,)]

            def ffn_pieces(b, g, turn):
                for n in SHARES[b]:
                    item = ITEM_FFN + FFN_PIECES * g + n
                    pool.wait_ge(w_hi, 2 * FFN_PIECES * turn + (item + 1))
                    weight_lo(row_ffn(g) + n, landing(item))

            pool.memset(minus_half[:], -0.5).then_inc(half_set, 1)
            pool.wait_ge(half_set, 1)
            first_norm1()
            matrix_lo(ITEM_R, ROW_R, range(3))
            operand_lo("r", 0, range(1))
            matrix_lo(ITEM_R, ROW_R, range(3, KT))
            operand_lo("r", 0, range(1, KT))
            norm1(1)
            matrix_lo(ITEM_K, ROW_K)
            operand_lo("k", 0)
            norm1(2)
            for b in range(1, BLOCKS):
                operand_lo("r", b)
                operand_lo("k", b)
                if b < 3:
                    matrix_lo((ITEM_V, ITEM_O)[b - 1], (ROW_V, ROW_O)[b - 1])
                if b + 2 < BLOCKS:
                    norm1(b + 2)
            operand_lo("v", 0)
            operand_lo("v", 1)
            operand_lo("y", 0)
            operand_lo("v", 2)
            operand_lo("y", 1)
            operand_lo("v", 3)
            matrix_lo(ITEM_CR, ROW_CR)
            operand_lo("y", 2)
            norm(BLOCKS)
            operand_lo("y", 3)
            norm(BLOCKS + 1)
            x_added(0)
            operand_lo("cr", 0)
            x_added(1)
            operand_lo("ck", 0)
            norm(BLOCKS + 2)
            operand_lo("cr", 1)
            x_added(2)
            operand_lo("ck", 1)
            norm(BLOCKS + 3)
            x_added(3)
            operand_lo("cr", 2)
            operand_lo("ck", 2)
            operand_lo("cr", 3)
            matrix_lo(ITEM_CM, row_cm(0), range(GROUP))
            operand_lo("ck", 3)
            matrix_lo(ITEM_CM, row_cm(0), range(GROUP, CM_PIECES))
            for v in range(2):
                inner_lo_tiles(v, 0)
                channel_piece(v, 0)
            with pool.Fori(0, TURNS) as turn:
                for v in range(2, PAIR + 2):
                    inner_lo_tiles(v, turn)
                    channel_piece(v, turn)
            for v in range(UNITS - PAIR + 2, UNITS - BLOCKS):
                inner_lo_tiles(v, 0)
                channel_piece(v, 0)
            inner_lo_tiles(UNITS - 4, 0)
            ffn_pieces(0, 0, 0)
            inner_lo_tiles(UNITS - 3, 0)
            ffn_pieces(1, 0, 0)
            norm(2 * BLOCKS)
            inner_lo_tiles(UNITS - 2, 0)
            ffn_pieces(2, 0, 0)
            norm(2 * BLOCKS + 1)
            inner_lo_tiles(UNITS - 1, 0)
            ffn_pieces(3, 0, 0)
            norm(2 * BLOCKS + 2)
            ffn_lo_tiles(0, 0)
            ffn_pieces(0, 1, 0)
            norm(2 * BLOCKS + 3)
            ffn_lo_tiles(1, 0)
            ffn_pieces(1, 1, 0)
            with pool.Fori(0, TURNS) as turn:
                for v in range(2, PAIR + 2):
                    ffn_lo_tiles(v, turn)
                    ffn_pieces(v % BLOCKS, v // BLOCKS + 1, turn)
            for v in range(UNITS - PAIR + 2, UNITS):
                ffn_lo_tiles(v, 0)
                if v < UNITS - BLOCKS:
                    ffn_pieces(v % BLOCKS, v // BLOCKS + 1, 0)


def kernel(**inputs):
    import numpy as np
    import concourse.bacc as bacc
    from concourse.bass_utils import run_bass_kernel_spmd

    def take(name):
        return np.asarray(inputs["L0_" + name])

    def feature_pieces(w):
        wt = w.T.reshape(KT, P, w.shape[0])
        if w.shape[0] == H:
            return list(wt)
        return [np.concatenate([wt[k], wt[k + 1]], axis=1) for k in range(0, KT, 2)]

    def inner_pieces(w):
        return list(w.T.reshape(GROUP, P, H))

    pieces = []
    for name in ("Wr", "Wk", "Wv", "Wo", "Wcr"):
        pieces += feature_pieces(take("attn_" + name))
    width = GROUP * P
    w_key, w_value = take("attn_Wkey"), take("attn_Wval")
    w_gate_up, w_down = take("ffn_w_gate_up"), take("ffn_w_down")
    for g in range(GROUPS):
        cut = slice(g * width, (g + 1) * width)
        pieces += feature_pieces(w_key[cut]) + inner_pieces(w_value[:, cut])
    for g in range(GROUPS):
        cut, up = slice(g * width, (g + 1) * width), slice(INNER + g * width, INNER + (g + 1) * width)
        pieces += feature_pieces(w_gate_up[cut]) + feature_pieces(w_gate_up[up]) + inner_pieces(w_down[:, cut])
    vectors = np.stack([take("attn_" + name).reshape(KT, P) for name in VECTORS])

    arrays = {
        "x": np.ascontiguousarray(take("attn_x")),
        "wts": np.ascontiguousarray(np.stack(pieces)),
        "vectors": np.ascontiguousarray(vectors.transpose(2, 0, 1)),
        "identity": np.eye(P, dtype=np.float32),
    }
    nc = bacc.Bacc("TRN2", target_bir_lowering=False, num_devices=1)
    args = [nc.dram_tensor(name, a.shape, F32, kind="ExternalInput").ap() for name, a in arrays.items()]
    out = nc.dram_tensor("out", (1, TOKENS, H), F32, kind="ExternalOutput").ap()
    build(nc, *args, out)
    r = run_bass_kernel_spmd(nc, [arrays], core_ids=[0])
    return r.results[0]["out"]
```
